# Optimizing a Trainium2 kernel written in Bass

```python
import numpy as np
import jax
import jax.numpy as jnp

def _softmax(x, axis=-1):
    return jax.nn.softmax(x, axis=axis)

def _gelu(x):
    return jax.nn.gelu(x, approximate=True)

def _silu(x):
    return jax.nn.silu(x)

def _sigmoid(x):
    return jax.nn.sigmoid(x)

def _layernorm(x, axis=-1, eps=1e-05):
    m = jnp.mean(x, axis=axis, keepdims=True)
    v = jnp.var(x, axis=axis, keepdims=True)
    return (x - m) / jnp.sqrt(v + eps)

def _scatter_add(tgt, idx, src, axis=0):
    return tgt.at[idx].add(src)

def _segment_sum(src, seg, n):
    return jax.ops.segment_sum(src, seg, n)
kernel_name = 'mk_decoder_postln_d1_seqx_r8_c1697f'

def setup_inputs(seed: int=0):
    np.random.seed(seed)
    _w = jnp.asarray

    def _rec_inputs():
        import jax
        import jax.numpy as jnp
        _rk = jax.random.key(seed)
        x = 7.22e-05 + 1 * jax.random.normal(jax.random.fold_in(_rk, 1), (8, 128, 128), jnp.float32)
        _lenS = 128 - jax.random.randint(jax.random.fold_in(_rk, 7), (8,), 0, max(1, 128 // 4) + 1, jnp.int32)
        _lenS2 = 128 - jax.random.randint(jax.random.fold_in(_rk, 8), (8,), 0, max(1, 128 // 4) + 1, jnp.int32)
        _ctx_1024P = jax.random.normal(jax.random.fold_in(_rk, 11), (8, 16, 128), jnp.float32)
        _ctx_1024c = jax.random.dirichlet(jax.random.fold_in(_rk, 511), 0.3 * jnp.ones((16,), jnp.float32), (8, 128))
        _ctx_1024t = jnp.einsum('bsk,bkd->bsd', _ctx_1024c, _ctx_1024P)
        _ctx_1024t = _ctx_1024t * jax.lax.rsqrt(jnp.mean(jnp.square(_ctx_1024t)) + 1e-12) * 0.953939
        ctx_1024 = 4.13588e-05 + 0.999923 * (_ctx_1024t + 0.3 * jax.random.normal(jax.random.fold_in(_rk, 611), (8, 128, 128), jnp.float32))
        _validS = jnp.arange(128)[None, :] < _lenS[:, None]
        _validS2 = jnp.arange(128)[None, :] < _lenS2[:, None]
        _causal = jnp.tril(jnp.ones((128, 128), dtype=bool))
        mask_BxS2_ff0 = jnp.where(jnp.ones((8, 128), dtype=bool), 0.0, -1000000000.0).astype(jnp.float32)
        return (x, ctx_1024, mask_BxS2_ff0)
    x, ctx_1024, mask_BxS2_ff0 = _rec_inputs()

    def _L0_attn_setup():
        import jax, jax.numpy as jnp
        import numpy as np
        from jax import lax
        D_MODEL = 128
        KERNEL = 7
        RMS_EPS = 1.1920929e-07

        def _depthwise_conv1d(x_bds, w, b):
            D = x_bds.shape[1]
            pad = w.shape[-1] // 2
            y = lax.conv_general_dilated(x_bds, w, window_strides=(1,), padding=[(pad, pad)], feature_group_count=D, dimension_numbers=('NCH', 'OIH', 'NCH'))
            return y + b[None, :, None]

        def _decay_scan(gated, decay):
            a = jnp.broadcast_to(decay[None, :, None], gated.shape)

            def combine(c1, c2):
                a1, b1 = c1
                a2, b2 = c2
                return (a1 * a2, a2 * b1 + b2)
            _, h = lax.associative_scan(combine, (a, gated), axis=2)
            return h
        key = jax.random.key(seed)
        ks = jax.random.split(key, 6)
        B, S, D, K = (4, 512, D_MODEL, KERNEL)
        x = jax.random.normal(ks[0], (B, S, D), dtype=jnp.float32)
        gate_w = jax.random.normal(ks[1], (D, 1, K), dtype=jnp.float32) * 0.1
        gate_b = jnp.zeros((D,), dtype=jnp.float32)
        cand_w = jax.random.normal(ks[2], (D, 1, K), dtype=jnp.float32) * 0.1
        cand_b = jnp.zeros((D,), dtype=jnp.float32)
        log_decay = jnp.full((D,), np.log(0.1), dtype=jnp.float32)
        out_w = jax.random.normal(ks[3], (D, D), dtype=jnp.float32) * 0.02
        out_b = jnp.zeros((D,), dtype=jnp.float32)
        norm_w = jnp.ones((D,), dtype=jnp.float32)
        return {'x': x, 'gate_w': gate_w, 'gate_b': gate_b, 'cand_w': cand_w, 'cand_b': cand_b, 'log_decay': log_decay, 'out_w': out_w, 'out_b': out_b, 'norm_w': norm_w}
    _L0_attn_all = _L0_attn_setup()
    _L0_attn_in = {k: v for k, v in _L0_attn_all.items() if k in ('gate_w', 'gate_b', 'cand_w', 'cand_b', 'log_decay', 'out_w', 'out_b', 'norm_w')}
    del _L0_attn_all

    def _L0_xattn_setup():
        import jax, jax.numpy as jnp
        import numpy as np
        D_MODEL = 128
        N_HEAD = 16
        HEAD_DIM = D_MODEL // N_HEAD
        key = jax.random.key(seed)
        ks = jax.random.split(key, 12)
        B, S, D = (4, 256, D_MODEL)
        scale = 1.0 / np.sqrt(D)
        inp = {'q': jax.random.normal(ks[0], (B, S, D), jnp.float32), 'k': jax.random.normal(ks[1], (B, S, D), jnp.float32), 'v': jax.random.normal(ks[2], (B, S, D), jnp.float32), 'attention_mask': jnp.zeros((B, S), jnp.float32), 'Wq': jax.random.normal(ks[3], (D, D), jnp.float32) * scale, 'bq': jnp.zeros((D,), jnp.float32), 'Wk': jax.random.normal(ks[4], (D, D), jnp.float32) * scale, 'bk': jnp.zeros((D,), jnp.float32), 'Wv': jax.random.normal(ks[5], (D, D), jnp.float32) * scale, 'bv': jnp.zeros((D,), jnp.float32), 'Wp': jax.random.normal(ks[6], (D, D), jnp.float32) * scale, 'bp': jnp.zeros((D,), jnp.float32)}
        return inp
    _L0_xattn_all = _L0_xattn_setup()
    _L0_xattn_in = {k: v for k, v in _L0_xattn_all.items() if k in ('Wq', 'bq', 'Wk', 'bk', 'Wv', 'bv', 'Wp', 'bp')}
    del _L0_xattn_all

    def _L0_ffn_setup():
        import jax, jax.numpy as jnp
        import numpy as np
        H = 128
        I = 512
        E = 8
        K = 2
        B, S = (2, 256)

        def _moe_linear(x, router_w, expert_w):
            n_exp = router_w.shape[0]
            logits = x @ router_w.T
            vals, idx = jax.lax.top_k(logits, K)
            probs = jax.nn.softmax(vals, axis=-1)
            onehot = jax.nn.one_hot(idx, n_exp, dtype=x.dtype)
            combine = jnp.einsum('tk,tke->te', probs, onehot)
            out = jnp.zeros((x.shape[0], expert_w.shape[1]), x.dtype)
            for e in range(n_exp):
                out = out + combine[:, e:e + 1] * (x @ expert_w[e].T)
            return out
        key = jax.random.key(seed)
        ks = jax.random.split(key, 7)
        init = lambda k, shape, fan_in: jax.random.normal(k, shape, jnp.float32) / np.float32(np.sqrt(fan_in))
        return {'x': jax.random.normal(ks[0], (B, S, H), jnp.float32), 'router_gate': init(ks[1], (E, H), H), 'w_gate': init(ks[2], (E, I, H), H), 'router_up': init(ks[3], (E, H), H), 'w_up': init(ks[4], (E, I, H), H), 'router_down': init(ks[5], (E, I), I), 'w_down': init(ks[6], (E, H, I), I)}
    _L0_ffn_all = _L0_ffn_setup()
    _L0_ffn_in = {k: v for k, v in _L0_ffn_all.items() if k in ('router_gate', 'w_gate', 'router_up', 'w_up', 'router_down', 'w_down')}
    del _L0_ffn_all
    return {'x': x, 'ctx_1024': ctx_1024, 'mask_BxS2_ff0': mask_BxS2_ff0, 'L0_attn_gate_w': _L0_attn_in['gate_w'], 'L0_attn_gate_b': _L0_attn_in['gate_b'], 'L0_attn_cand_w': _L0_attn_in['cand_w'], 'L0_attn_cand_b': _L0_attn_in['cand_b'], 'L0_attn_log_decay': _L0_attn_in['log_decay'], 'L0_attn_out_w': _L0_attn_in['out_w'], 'L0_attn_out_b': _L0_attn_in['out_b'], 'L0_attn_norm_w': _L0_attn_in['norm_w'], 'L0_xattn_Wq': _L0_xattn_in['Wq'], 'L0_xattn_bq': _L0_xattn_in['bq'], 'L0_xattn_Wk': _L0_xattn_in['Wk'], 'L0_xattn_bk': _L0_xattn_in['bk'], 'L0_xattn_Wv': _L0_xattn_in['Wv'], 'L0_xattn_bv': _L0_xattn_in['bv'], 'L0_xattn_Wp': _L0_xattn_in['Wp'], 'L0_xattn_bp': _L0_xattn_in['bp'], 'L0_ffn_router_gate': _L0_ffn_in['router_gate'], 'L0_ffn_w_gate': _L0_ffn_in['w_gate'], 'L0_ffn_router_up': _L0_ffn_in['router_up'], 'L0_ffn_w_up': _L0_ffn_in['w_up'], 'L0_ffn_router_down': _L0_ffn_in['router_down'], 'L0_ffn_w_down': _L0_ffn_in['w_down']}

def reference(x, ctx_1024, mask_BxS2_ff0, L0_attn_gate_w, L0_attn_gate_b, L0_attn_cand_w, L0_attn_cand_b, L0_attn_log_decay, L0_attn_out_w, L0_attn_out_b, L0_attn_norm_w, L0_xattn_Wq, L0_xattn_bq, L0_xattn_Wk, L0_xattn_bk, L0_xattn_Wv, L0_xattn_bv, L0_xattn_Wp, L0_xattn_bp, L0_ffn_router_gate, L0_ffn_w_gate, L0_ffn_router_up, L0_ffn_w_up, L0_ffn_router_down, L0_ffn_w_down):
    import jax
    import jax.numpy as jnp

    def _L0_attn_ref(x, gate_w, gate_b, cand_w, cand_b, log_decay, out_w, out_b, norm_w):
        import jax, jax.numpy as jnp
        import numpy as np
        from jax import lax
        D_MODEL = 128
        KERNEL = 7
        RMS_EPS = 1.1920929e-07

        def _depthwise_conv1d(x_bds, w, b):
            D = x_bds.shape[1]
            pad = w.shape[-1] // 2
            y = lax.conv_general_dilated(x_bds, w, window_strides=(1,), padding=[(pad, pad)], feature_group_count=D, dimension_numbers=('NCH', 'OIH', 'NCH'))
            return y + b[None, :, None]

        def _decay_scan(gated, decay):
            a = jnp.broadcast_to(decay[None, :, None], gated.shape)

            def combine(c1, c2):
                a1, b1 = c1
                a2, b2 = c2
                return (a1 * a2, a2 * b1 + b2)
            _, h = lax.associative_scan(combine, (a, gated), axis=2)
            return h
        residual = x
        x_t = jnp.transpose(x, (0, 2, 1))
        gate = jax.nn.sigmoid(_depthwise_conv1d(x_t, gate_w, gate_b))
        cand = jnp.tanh(_depthwise_conv1d(x_t, cand_w, cand_b))
        gated = gate * cand
        decay = jnp.exp(log_decay)
        h = _decay_scan(gated, decay)
        h = jnp.transpose(h, (0, 2, 1))
        out = jnp.einsum('bsd,ed->bse', h, out_w) + out_b
        y = out + residual
        ms = jnp.mean(y * y, axis=-1, keepdims=True)
        return y * lax.rsqrt(ms + RMS_EPS) * norm_w

    def _L0_xattn_ref(q, k, v, attention_mask, Wq, bq, Wk, bk, Wv, bv, Wp, bp):
        import jax, jax.numpy as jnp
        import numpy as np
        D_MODEL = 128
        N_HEAD = 16
        HEAD_DIM = D_MODEL // N_HEAD
        B, S, D = q.shape
        H, Dh = (N_HEAD, HEAD_DIM)
        wq = (q @ Wq + bq).reshape(B, S, H, Dh).transpose(0, 2, 1, 3)
        wk = (k @ Wk + bk).reshape(B, S, H, Dh).transpose(0, 2, 1, 3)
        wv = (v @ Wv + bv).reshape(B, S, H, Dh).transpose(0, 2, 1, 3)
        scores = jnp.einsum('bhqd,bhkd->bhqk', wq, wk) / jnp.sqrt(jnp.asarray(Dh, wq.dtype))
        causal = jnp.tril(jnp.ones((S, S), bool))[None, None]
        mask_value = jnp.finfo(scores.dtype).min
        scores = jnp.where(causal, scores, mask_value)
        scores = scores + attention_mask[:, None, None, :]
        att = jax.nn.softmax(scores, axis=-1)
        out = jnp.einsum('bhqk,bhkd->bhqd', att, wv)
        out = out.transpose(0, 2, 1, 3).reshape(B, S, H * Dh)
        return out @ Wp + bp

    def _L0_ffn_ref(x, router_gate, w_gate, router_up, w_up, router_down, w_down):
        import jax, jax.numpy as jnp
        import numpy as np
        H = 128
        I = 512
        E = 8
        K = 2
        B, S = (2, 256)

        def _moe_linear(x, router_w, expert_w):
            n_exp = router_w.shape[0]
            logits = x @ router_w.T
            vals, idx = jax.lax.top_k(logits, K)
            probs = jax.nn.softmax(vals, axis=-1)
            onehot = jax.nn.one_hot(idx, n_exp, dtype=x.dtype)
            combine = jnp.einsum('tk,tke->te', probs, onehot)
            out = jnp.zeros((x.shape[0], expert_w.shape[1]), x.dtype)
            for e in range(n_exp):
                out = out + combine[:, e:e + 1] * (x @ expert_w[e].T)
            return out
        b, s, h = x.shape
        xt = x.reshape(b * s, h)
        g = _moe_linear(xt, router_gate, w_gate)
        u = _moe_linear(xt, router_up, w_up)
        inter = jax.nn.silu(g) * u
        d = _moe_linear(inter, router_down, w_down)
        return d.reshape(b, s, h)
    x = _layernorm(x + _L0_attn_ref(x, L0_attn_gate_w, L0_attn_gate_b, L0_attn_cand_w, L0_attn_cand_b, L0_attn_log_decay, L0_attn_out_w, L0_attn_out_b, L0_attn_norm_w), axis=-1)
    x = _layernorm(x + _L0_xattn_ref(x, ctx_1024, ctx_1024, mask_BxS2_ff0, L0_xattn_Wq, L0_xattn_bq, L0_xattn_Wk, L0_xattn_bk, L0_xattn_Wv, L0_xattn_bv, L0_xattn_Wp, L0_xattn_bp), axis=-1)
    x = _layernorm(x + _L0_ffn_ref(x, L0_ffn_router_gate, L0_ffn_w_gate, L0_ffn_router_up, L0_ffn_w_up, L0_ffn_router_down, L0_ffn_w_down), axis=-1)
    return x

_drawn_inputs = setup_inputs


def setup_inputs(seed=0):
    import zlib

    import numpy as np

    out = dict(_drawn_inputs(seed))
    spreads = {'L0_attn_gate_b': (0.0, 0.8),
     'L0_attn_cand_b': (0.0, 0.1),
     'L0_attn_log_decay': (-2.3025851249694824, 0.6),
     'L0_attn_out_b': (0.0, 0.1),
     'L0_attn_norm_w': (1.0, 0.2),
     'L0_xattn_bq': (0.0, 0.1),
     'L0_xattn_bk': (0.0, 0.8),
     'L0_xattn_bv': (0.0, 0.1),
     'L0_xattn_bp': (0.0, 0.1)}
    factors = {'L0_attn_gate_w': 3.466}
    for name, (base, spread) in spreads.items():
        noise = np.random.default_rng([zlib.crc32(name.encode()), seed]).standard_normal(out[name].shape)
        drawn = base * np.exp(spread * noise) if base else spread * noise
        out[name] = jnp.asarray(drawn.astype(out[name].dtype))
    for name, factor in factors.items():
        out[name] = (out[name] * factor).astype(out[name].dtype)
    return out
```

```python
from contextlib import ExitStack

import concourse.bass as bass
from concourse import mybir

F32 = mybir.dt.float32
F32R = mybir.dt.float32r
BF16 = mybir.dt.bfloat16
U32 = mybir.dt.uint32
ALU = mybir.AluOpType
ACT = mybir.ActivationFunctionType
AX_X = mybir.AxisListType.X

P = 128
B = 8
HB = 4
TAPS = 7
PAD = TAPS // 2
ROW = P + 2 * PAD
HEADS, DH = 16, 8
NG = 4
NS = 4
E = 8
I = 512
IC = I // P
SCALE = float(DH) ** -0.5
RMS_EPS = 1.1920929e-07
LN_EPS = 1e-05
WCH = 1024
NCH = 3 * E * I // WCH
CPW = E * I // WCH
CAUSAL = -3.3895313892515355e38

C_GW, C_CW, C_GB, C_CB, C_LD = 0, TAPS, 2 * TAPS, 2 * TAPS + 1, 2 * TAPS + 2
C_BQ = C_LD + 1
C_BK = C_BQ + NG
C_QONE = C_BK + NG
C_KONE = C_QONE + 1
C_QLOW = C_KONE + 1
C_KLOW = C_QLOW + 1
NCOL = C_KLOW + 1
R_OB, R_NW, R_BV, R_BP, R_HM, R_IO = 0, P, 2 * P, 3 * P, 4 * P, 4 * P + NS * P
NROW = R_IO + E
HI_HI, HI_LO, LO_HI, MASK_HI, MASK_LO, MAX_HI, MAX_LO = 0, DH, 2 * DH, 3 * DH, 3 * DH + 1, 3 * DH + 2, 3 * DH + 3


def decoder_layer(nc, x_tok, x_t, ctx_t, mask, cols, rows, out_w, w_q, w_k, w_v, w_p, mask_rows,
                  r_gu, r_down, w_gate, w_up, w_down, out):
    with ExitStack() as ctx:
        def sb(name, shape, dt=F32):
            return ctx.enter_context(nc.sbuf_tensor(name, shape, dt))

        def sem(name):
            return ctx.enter_context(nc.semaphore(name))

        XT = sb("XT", [P, B, ROW])
        X = sb("X", [P, B, P])
        CT = sb("CT", [P, B * P])
        MK = sb("MK", [1, B * P])
        EK = sb("EK", [1, P])
        CO = sb("CO", [P, NCOL])
        RO = sb("RO", [P, NROW])
        OW = sb("OW", [P, P])
        WQ = sb("WQ", [P, NG, P])
        WK = sb("WK", [P, NG, P])
        WV = sb("WV", [P, P])
        WP = sb("WP", [P, P])
        RGU = sb("RGU", [P, 2 * E])
        RD = sb("RD", [P, IC * E])
        RDH = sb("RDH", [P, IC * E], F32R)
        RDL = sb("RDL", [P, IC * E], F32R)
        ID = sb("ID", [P, P])
        IDB = sb("IDB", [P, P], BF16)
        CM = sb("CM", [P, P], BF16)
        DIAG = sb("DIAG", [P, TAPS, P])
        DEC = sb("DEC", [P, 1])
        HGB = sb("HGB", [P, 1])
        BQ = sb("BQ", [P, NG])
        BK = sb("BK", [P, NG])
        BQL = sb("BQL", [P, NG])
        BKL = sb("BKL", [P, NG])
        MHALF = sb("MHALF", [P, 2 * HB])
        WH = sb("WH", [P, 3, E * I], F32R)
        WL = sb("WL", [P, 3, E * I], F32R)
        RAW = sb("RAW", [P, 2, WCH])
        ACC = sb("ACC", [P, HB, P])
        TG = sb("TG", [P, HB * P])
        TC = sb("TC", [P, HB * P])
        HT = sb("HT", [P, HB * P])
        XB = sb("XB", [P, HB * P])
        Y = sb("Y", [P, HB * P])
        SQ = sb("SQ", [P, P])
        MS = sb("MS", [P, HB])
        RS = sb("RS", [P, HB])
        ST6 = sb("ST6", [P, HB, 6])
        MV = sb("MV", [P, HB, 2])
        RSTD = sb("RSTD", [P, HB])
        X1 = sb("X1", [P, HB * P])
        X1T = sb("X1T", [P, HB * P])
        X1B = sb("X1B", [P, HB * P])
        LOW = sb("LOW", [P, 2, HB * P], F32R)
        QS = sb("QS", [P, NG, HB * P], F32R)
        KS = sb("KS", [P, NG, HB * P], F32R)
        QSA = sb("QSA", [P, NG, P], F32R)
        VB = sb("VB", [P, HB, P])
        VM = sb("VM", [P, HB, NS, P])
        NM = sb("NM", [P, NS, NG])
        NMS = sb("NMS", [P, NG, P])
        PT = sb("PT", [P, NS, NG, P])
        RC = sb("RC", [P, P])
        OT = sb("OT", [P, P])
        Z = sb("Z", [P, HB * P])
        X2 = sb("X2", [P, B, P])
        LG = sb("LG", [P, 2 * HB, E])
        V8 = sb("V8", [P, 2 * HB, 8])
        I8 = sb("I8", [P, 2 * HB, 8], U32)
        IF = sb("IF", [P, 2 * HB, 2])
        DV = sb("DV", [P, 2 * HB])
        EX = sb("EX", [P, 2 * HB])
        SM = sb("SM", [P, 2 * HB])
        P0 = sb("P0", [P, 2 * HB])
        P1 = sb("P1", [P, 2 * HB])
        OH = sb("OH", [P, 2 * HB, E])
        CGU = sb("CGU", [P, B, 2, E])
        XE = [PT[:, 2 * r:2 * r + 2, :, :].rearrange("p a g t -> p (a g) t") for r in range(2)]
        XH = [S[:, 0:2, :].rearrange("p a c -> p (a c)") for S in (QS, KS)]
        XL = [S[:, 2:4, :].rearrange("p a c -> p (a c)") for S in (QS, KS)]
        TH = TG
        SG = TC
        INT = HT
        ITH, ITL = LOW[:, 0, :], LOW[:, 1, :]
        DLG = sb("DLG", [P, E])
        DV8 = sb("DV8", [P, 8])
        DI8 = sb("DI8", [P, 8], U32)
        DIF = sb("DIF", [P, 2])
        DD = sb("DD", [P, 1])
        DE = sb("DE", [P, 1])
        DS = sb("DS", [P, 1])
        DP = sb("DP", [P, 2])
        DC = sb("DC", [P, 2, E])
        CD = sb("CD", [P, E])
        YD = sb("YD", [P, 2, P])
        S6 = sb("S6", [P, 6])
        M2 = sb("M2", [P, 2])
        R1 = sb("R1", [P, 1])
        OUT = sb("OUT", [P, 2, P])

        PS = ctx.enter_context(nc.psum_tensor("PS", [P, 8, 512], F32))

        ld_x = sem("ld_x")
        ld_k = sem("ld_k")
        ld_t = sem("ld_t")
        ld_q = sem("ld_q")
        ld_w = [sem("ld_w0"), sem("ld_w1")]
        c_id = sem("c_id")
        c_dve = sem("c_dve")
        c_act = sem("c_act")
        dv = sem("dv")
        pl = sem("pl")
        w_hi = sem("w_hi")
        w_lo = sem("w_lo")
        pe_gc = sem("pe_gc"); pe_p = sem("pe_p"); pe_v = sem("pe_v"); pe_o = sem("pe_o")
        pe_x1 = sem("pe_x1"); pe_s = sem("pe_s"); pe_aug = sem("pe_aug"); pe_st = sem("pe_st")
        pe_pv = sem("pe_pv"); pe_wo = sem("pe_wo"); pe_x2 = sem("pe_x2"); pe_lg = sem("pe_lg")
        a_tg = sem("a_tg"); a_tc = sem("a_tc"); a_low = sem("a_low"); a_ms = sem("a_ms")
        a_x1 = sem("a_x1"); a_exp = sem("a_exp"); a_x2 = sem("a_x2"); a_ex = sem("a_ex")
        d_cand = sem("d_cand"); d_vb = sem("d_vb"); d_st = sem("d_st"); d_ht = sem("d_ht")
        d_y = sem("d_y"); d_mv = sem("d_mv"); d_x1 = sem("d_x1"); d_max = sem("d_max")
        d_nms = sem("d_nms"); d_qsa = sem("d_qsa"); d_ot = sem("d_ot"); d_z = sem("d_z")
        d_mv2 = sem("d_mv2"); d_x2 = sem("d_x2"); d_dv = sem("d_dv"); d_cgu = sem("d_cgu")
        p_xb = sem("p_xb"); p_rs = sem("p_rs"); p_r1 = sem("p_r1"); p_x1b = sem("p_x1b")
        p_vm = sem("p_vm"); p_sel = sem("p_sel"); p_r2 = sem("p_r2")
        f_xe = [sem("f_xe0"), sem("f_xe1")]
        f_t = sem("f_t"); f_h = sem("f_h"); f_l = sem("f_l")
        f_g = sem("f_g"); f_u = sem("f_u"); f_th = sem("f_th"); f_int = sem("f_int")
        f_it = sem("f_it"); f_ith = sem("f_ith"); f_itl = sem("f_itl"); f_ld = sem("f_ld")
        f_dd = sem("f_dd"); f_de = sem("f_de"); f_lg = sem("f_lg")
        f_dn = sem("f_dn"); f_acc = sem("f_acc"); f_mv = sem("f_mv"); f_r = sem("f_r")
        f_out = sem("f_out")
        st = [sem("st0"), sem("st1")]

        block = ctx.enter_context(nc.Block())
        NLX, NLK, NLT = 2 * 16, 6 * 16, 4 * 16

        def flat(ap):
            return ap.rearrange("p a b -> p (a b)")

        w_src = [w_gate, w_up, w_down]

        @block.sync
        def _(sp):
            sp.dma_start(XT[:, :, PAD:PAD + P], x_t).then_inc(ld_x, 16)
            sp.dma_start(CO[:, :], cols).then_inc(ld_x, 16)
            sp.dma_start(CT[:, :], ctx_t).then_inc(ld_k, 16)
            sp.dma_start(WK[:, :, :], w_k).then_inc(ld_k, 16)
            sp.dma_start(MK[:, :], mask).then_inc(ld_k, 16)
            sp.dma_start(EK[:, :], mask_rows).then_inc(ld_k, 16)
            sp.dma_start(WV[:, :], w_v).then_inc(ld_k, 16)
            sp.dma_start(RO[:, :], rows.partition_broadcast(P)).then_inc(ld_k, 16)
            for c in range(NCH):
                if c >= 2:
                    sp.wait_ge(w_lo, c - 1)
                sp.dma_start(RAW[:, c % 2, :], w_src[c // CPW][:, (c % CPW) * WCH:(c % CPW + 1) * WCH])\
                    .then_inc(ld_w[c % 2], 16)
            for t in range(B):
                sp.wait_ge(f_out, t + 1)
                sp.dma_start(out[t], OUT[:, t % 2, :]).then_inc(st[t % 2], 16)
            for q in st:
                sp.wait_ge(q, 16 * B // 2)

        @block.gpsimd
        def _(pool):
            np_ = [0]

            def step(ins):
                np_[0] += 1
                ins.then_inc(pl, 1)
                return np_[0]

            g = nc.gpsimd
            g.memset(XT[:, :, 0:PAD], 0.0)
            g.memset(XT[:, :, PAD + P:ROW], 0.0).then_inc(c_id, 1)
            a = step(g.memset(ID[:, :], 0.0))
            b = step(g.memset(CM[:, :], 0.0))
            pool.wait_ge(pl, b)
            a = step(g.affine_select(out=ID[:, :], in_=ID[:, :], compare_op=ALU.not_equal, fill=1.0, base=0,
                                     pattern=[[-1, P]], channel_multiplier=1))
            g.affine_select(out=CM[:, :], in_=CM[:, :], compare_op=ALU.is_ge, fill=CAUSAL, base=0,
                            pattern=[[-1, P]], channel_multiplier=1).then_inc(c_id, 1)
            pool.wait_ge(pl, a)
            g.tensor_copy(IDB[:, :], ID[:, :]).then_inc(c_id, 1)
            pool.wait_ge(ld_x, NLX)
            for k in range(TAPS):
                g.tensor_scalar(DIAG[:, k, :], ID[:, :], CO[:, C_GW + k:C_GW + k + 1], None, ALU.mult)\
                    .then_inc(c_id, 1)
            g.memset(NMS[:, :, :], 0.0)
            g.memset(MHALF[:, :], -0.5).then_inc(c_id, 1)
            pool.wait_ge(c_id, TAPS + 4)
            g.tensor_scalar(HGB[:, :], CO[:, C_GB:C_GB + 1], 0.5, None, ALU.mult).then_inc(c_id, 1)

            def inv_sqrt(dst, src, scale, eps, n):
                c = step(g.tensor_scalar(dst, src, scale, eps, ALU.mult, ALU.add))
                pool.wait_ge(pl, c)
                return g.tensor_tensor(dst, dst, MHALF[:, 0:n], ALU.pow)

            def split_low(c):
                w, o = c // CPW, (c % CPW) * WCH
                pool.wait_ge(w_hi, c + 1)
                g.tensor_tensor(WL[:, w, o:o + WCH], RAW[:, c % 2, :], WH[:, w, o:o + WCH].bitcast(F32),
                                ALU.subtract).then_inc(w_lo, 1)

            for h in range(2):
                if h == 0:
                    pool.wait_ge(ld_t, NLT)
                    pool.wait_ge(ld_k, NLK)
                else:
                    pool.wait_ge(d_y, h)
                g.tensor_tensor(XB[:, :].rearrange("p (b t) -> p b t", b=HB), X[:, HB * h:HB * h + HB, :],
                                RO[:, None, R_OB:R_OB + P].broadcast_to([P, HB, P]), ALU.add).then_inc(p_xb, 1)
                pool.wait_ge(d_vb, h + 1)
                if h:
                    pool.wait_ge(pe_pv, HB * h)
                for i in range(HB):
                    g.tensor_tensor(VM[:, i, :, :], VB[:, i, None, :].broadcast_to([P, NS, P]),
                                    RO[:, R_HM:R_HM + NS * P].rearrange("p (s d) -> p s d", s=NS),
                                    ALU.mult).then_inc(p_vm, 1)
                for c in range(6 * h, 6 * h + 2):
                    split_low(c)
                pool.wait_ge(a_ms, HB * (h + 1))
                inv_sqrt(RS[:, :], MS[:, :], 1.0 / P, RMS_EPS, HB).then_inc(p_rs, 1)
                pool.wait_ge(d_mv, h + 1)
                inv_sqrt(RSTD[:, :], MV[:, :, 1], 1.0, LN_EPS, HB).then_inc(p_r1, 1)
                pool.wait_ge(d_x1, HB * (h + 1))
                if h:
                    pool.wait_ge(d_z, HB * h)
                g.tensor_tensor(X1B[:, :].rearrange("p (b t) -> p b t", b=HB),
                                X1[:, :].rearrange("p (b t) -> p b t", b=HB),
                                RO[:, None, R_BP:R_BP + P].broadcast_to([P, HB, P]), ALU.add).then_inc(p_x1b, 1)
                for i in range(HB):
                    t = HB * h + i
                    for p in range(2):
                        pool.wait_ge(a_exp, 2 * t + p + 1)
                        v = PT[:, 2 * p:2 * p + 2, :, :].rearrange("k s g q -> k (s g) q")
                        g.affine_select(out=v, in_=v, compare_op=ALU.is_ge, fill=0.0, base=0,
                                        pattern=[[0, 2 * NG], [1, P]], channel_multiplier=-1).then_inc(p_sel, 1)
                    split_low(6 * h + 2 + i)
                pool.wait_ge(d_mv2, h + 1)
                inv_sqrt(RSTD[:, :], MV[:, :, 1], 1.0, LN_EPS, HB).then_inc(p_r2, 1)

            def spread(t, r):
                if t:
                    pool.wait_ge(f_t, 4 * (t - 1) + 2 * r + 2)
                g.tensor_tensor(XE[r], X2[:, t, None, :].broadcast_to([P, E, P]),
                                CGU[:, t, r, :, None].broadcast_to([P, E, P]), ALU.mult).then_inc(f_xe[r], 1)

            pool.wait_ge(d_cgu, 2)
            pool.wait_ge(pe_lg, 2)
            for r in range(2):
                spread(0, r)
            for t in range(B):
                if t + 1 < B:
                    for r in range(2):
                        spread(t + 1, r)
                if t >= 1:
                    pool.wait_ge(f_mv, t)
                    inv_sqrt(R1[:, :], M2[:, 1:2], 1.0, LN_EPS, 1).then_inc(f_r, 1)
            pool.wait_ge(f_mv, B)
            inv_sqrt(R1[:, :], M2[:, 1:2], 1.0, LN_EPS, 1).then_inc(f_r, 1)

        @block.scalar
        def _(act):
            s = nc.scalar
            act.dma_start(X[:, :, :], x_tok).then_inc(ld_t, 16)
            act.dma_start(OW[:, :], out_w).then_inc(ld_t, 16)
            act.dma_start(RGU[:, :], r_gu).then_inc(ld_t, 16)
            act.dma_start(RD[:, :], r_down).then_inc(ld_t, 16)
            act.dma_start(WQ[:, :, :], w_q).then_inc(ld_q, 16)
            act.dma_start(WP[:, :], w_p).then_inc(ld_q, 16)
            act.wait_ge(ld_x, NLX)
            s.activation(DEC[:, :], CO[:, C_LD:C_LD + 1], ACT.Exp).then_inc(c_act, 1)

            def split_high(c):
                w, o = c // CPW, (c % CPW) * WCH
                act.wait_ge(ld_w[c % 2], 16 * (c // 2 + 1))
                s.copy(WH[:, w, o:o + WCH], RAW[:, c % 2, :]).then_inc(w_hi, 1)

            def low_rows(j, low, bias):
                act.wait_ge(pe_p, j + 1)
                if j >= 2:
                    act.wait_ge(d_st, j - 1)
                s.activation(LOW[:, j % 2, :], PS[:, 4 + j % 2, :], ACT.Identity, bias=bias, scale=low)\
                    .then_inc(a_low, 1)

            for h in range(2):
                act.wait_ge(pe_gc, h + 1)
                act.wait_ge(c_id, TAPS + 5)
                s.activation(TG[:, :], PS[:, 6, :], ACT.Tanh, bias=HGB[:, :], scale=0.5).then_inc(a_tg, 1)
                act.wait_ge(c_dve, 4)
                for g in range(NG):
                    low_rows(8 * h + g, CO[:, C_KLOW:C_KLOW + 1], BKL[:, g:g + 1])
                act.wait_ge(d_cand, h + 1)
                s.activation(TC[:, :], flat(ACC[:, :, :]), ACT.Tanh, bias=CO[:, C_CB:C_CB + 1]).then_inc(a_tc, 1)
                for c in range(6 * h, 6 * h + 2):
                    split_high(c)
                act.wait_ge(d_y, h + 1)
                for i in range(HB):
                    if i or h:
                        act.wait_ge(a_ms, HB * h + i)
                    s.activation(SQ[:, :], Y[:, i * P:(i + 1) * P], ACT.Square, accum_out=MS[:, i:i + 1])\
                        .then_inc(a_ms, 1)
                act.wait_ge(pe_x1, h + 1)
                s.copy(X1T[:, :], PS[:, 6, :]).then_inc(a_x1, 1)
                for g in range(NG):
                    low_rows(8 * h + 4 + g, CO[:, C_QLOW:C_QLOW + 1], BQL[:, g:g + 1])
                for i in range(HB):
                    t = HB * h + i
                    for p in range(2):
                        act.wait_ge(pe_st, 2 * t + p + 1)
                        s.activation(PT[:, 2 * p:2 * p + 2, :, :].rearrange("k s g q -> k (s g q)"),
                                     PS[:, 4:6, :].rearrange("k s c -> k (s c)"), ACT.Exp).then_inc(a_exp, 1)
                    split_high(6 * h + 2 + i)
                act.wait_ge(pe_x2, h + 1)
                s.copy(X1T[:, :], PS[:, 6, :]).then_inc(a_x2, 1)
                act.wait_ge(d_dv, h + 1)
                s.activation(EX[:, :], DV[:, :], ACT.Exp).then_inc(a_ex, 1)

            def high(k):
                t, r, q = k // 4, k // 2 % 2, k % 2
                act.wait_ge(f_t, k + 1)
                s.copy(XH[r][:, q * 512:q * 512 + 512], PS[:, k % 2, :]).then_inc(f_h, 1)

            for k in range(4):
                high(k)
            for t in range(B + 1):
                if t < B:
                    act.wait_ge(f_g, t + 1)
                    s.activation(TH[:, :], PS[:, 2, :], ACT.Tanh, scale=0.5).then_inc(f_th, 1)
                if t + 1 < B:
                    for k in range(4 * t + 4, 4 * t + 6):
                        high(k)
                if t >= 1:
                    act.wait_ge(f_dd, t)
                    s.activation(DE[:, :], DD[:, :], ACT.Exp).then_inc(f_de, 1)
                if t + 1 < B:
                    for k in range(4 * t + 6, 4 * t + 8):
                        high(k)
                if t < B:
                    act.wait_ge(f_it, t + 1)
                    s.copy(ITH[:, :], PS[:, 6, :]).then_inc(f_ith, 1)

        @block.tensor
        def _(pe):
            mm = nc.tensor.matmul
            for h in range(2):
                if h == 0:
                    pe.wait_ge(ld_x, NLX)
                    pe.wait_ge(c_id, TAPS + 3)
                else:
                    pe.wait_ge(a_x2, h)
                for k in range(TAPS):
                    last = mm(PS[:, 6, :].rearrange("p (b t) -> p b t", b=HB), DIAG[:, k, :],
                              XT[:, HB * h:HB * h + HB, k:k + P], start=k == 0, stop=k == TAPS - 1)
                last.then_inc(pe_gc, 1)
                if h == 0:
                    pe.wait_ge(ld_k, NLK)
                else:
                    pe.wait_ge(a_exp, 2 * HB * h)
                for g in range(NG):
                    j = 8 * h + g
                    if g >= 2:
                        pe.wait_ge(d_st, j - 1)
                    mm(PS[:, 4 + g % 2, :], WK[:, g, :], CT[:, HB * P * h:HB * P * (h + 1)], start=True, stop=False)
                    mm(PS[:, 4 + g % 2, :], EK[0:1, :], MK[0:1, HB * P * h:HB * P * (h + 1)], start=False, stop=True)\
                        .then_inc(pe_p, 1)
                if h:
                    pe.wait_ge(d_cgu, h)
                for i in range(HB):
                    b = HB * h + i
                    last = mm(PS[:, 7, i * P:(i + 1) * P], CT[:, b * P:(b + 1) * P], WV[:, :], start=True, stop=True)
                last.then_inc(pe_v, 1)
                pe.wait_ge(ld_t, NLT)
                pe.wait_ge(d_vb, h + 1)
                for i in range(HB):
                    pe.wait_ge(d_ht, HB * h + i + 1)
                    last = mm(PS[:, 7, i * P:(i + 1) * P], HT[:, i * P:(i + 1) * P], OW[:, :], start=True, stop=True)
                last.then_inc(pe_o, 1)
                pe.wait_ge(a_tg, h + 1)
                for i in range(HB):
                    pe.wait_ge(d_x1, HB * h + i + 1)
                    last = nc.tensor.transpose(PS[:, 6, i * P:(i + 1) * P], X1[:, i * P:(i + 1) * P], ID[:, :])
                last.then_inc(pe_x1, 1)
                pe.wait_ge(a_x1, h + 1)
                pe.wait_ge(c_dve, 4)
                for g in range(NG):
                    pe.wait_ge(d_st, 8 * h + 3 + g)
                    mm(PS[:, 4 + g % 2, :], WQ[:, g, :], X1T[:, :], start=True, stop=True).then_inc(pe_p, 1)

                def scores(i):
                    for s in range(NS):
                        if s % 2 == 0 and HB * h + i:
                            pe.wait_ge(d_max, 2 * (HB * h + i - 1) + s // 2 + 1)
                        mm(PS[:, s, :].rearrange("p (g k) -> p g k", g=NG), IDB[:, :],
                           CM[:, None, :].broadcast_to([P, NG, P]), start=True, stop=False, skip_group_check=True)
                    for p in range(2):
                        for g in range(NG):
                            for s in range(2 * p, 2 * p + 2):
                                last = mm(PS[:, s, g * P:(g + 1) * P],
                                          QS[32 * s:32 * s + 32, g, i * P:(i + 1) * P],
                                          KS[32 * s:32 * s + 32, g, i * P:(i + 1) * P],
                                          start=False, stop=g == NG - 1, skip_group_check=True)
                        last.then_inc(pe_s, 1)

                def scores_t(i, p):
                    if HB * h + i or p:
                        pe.wait_ge(a_exp, 2 * (HB * h + i) + p)
                    for g in range(NG):
                        for s in range(2 * p, 2 * p + 2):
                            last = mm(PS[:, 4 + s % 2, g * P:(g + 1) * P], KS[32 * s:32 * s + 32, g, i * P:(i + 1) * P],
                                      QSA[32 * s:32 * s + 32, g, :], start=True, stop=True)
                    last.then_inc(pe_st, 1)

                def values(i):
                    t = HB * h + i
                    pe.wait_ge(p_vm, HB * (h + 1))
                    pe.wait_ge(p_sel, 2 * t + 2)
                    if i == 0:
                        pe.wait_ge(d_y, h + 1)
                    else:
                        pe.wait_ge(d_z, t)
                    for s in range(NS):
                        for g in range(NG):
                            mm(PS[32 * g:32 * g + 32, 7, 0:P], VM[:, i, s, 32 * g:32 * g + 32], PT[:, s, g, :],
                               start=s == 0, stop=s == NS - 1, skip_group_check=True)
                        for g in range(NG):
                            last = mm(PS[32 * g:32 * g + 32, 7, P:2 * P],
                                      RO[:, R_HM + s * P + 32 * g:R_HM + s * P + 32 * g + 32], PT[:, s, g, :],
                                      start=False, stop=s == NS - 1, skip_group_check=True)
                    last.then_inc(pe_pv, 1)

                def project(i):
                    pe.wait_ge(d_ot, HB * h + i + 1)
                    mm(PS[:, 7, 2 * P:3 * P], OT[:, :], WP[:, :], start=True, stop=True).then_inc(pe_wo, 1)

                pe.wait_ge(d_st, 8 * h + 8)
                scores(0)
                for i in range(HB + 1):
                    t = HB * h + i
                    if i < HB:
                        pe.wait_ge(d_nms, t + 1)
                        if i:
                            pe.wait_ge(d_qsa, t)
                        for g in range(NG):
                            last = nc.tensor.transpose(PS[:, 6, g * P:(g + 1) * P], NMS[:, g, :], ID[:, :])
                        last.then_inc(pe_aug, 1)
                    if i:
                        values(i - 1)
                    if i < HB:
                        pe.wait_ge(d_qsa, t + 1)
                        scores_t(i, 0)
                    if i:
                        project(i - 1)
                    if i + 1 < HB:
                        scores(i + 1)
                    if i < HB:
                        scores_t(i, 1)
                for i in range(HB):
                    pe.wait_ge(d_x2, HB * h + i + 1)
                    last = nc.tensor.transpose(PS[:, 6, i * P:(i + 1) * P], X2[:, HB * h + i, :], ID[:, :])
                last.then_inc(pe_x2, 1)
                pe.wait_ge(a_x2, h + 1)
                for i in range(HB):
                    last = mm(PS[:, 7, 2 * E * i:2 * E * (i + 1)], X1T[:, i * P:(i + 1) * P], RGU[:, :],
                              start=True, stop=True)
                last.then_inc(pe_lg, 1)

            def turn(k):
                t, r, q = k // 4, k // 2 % 2, k % 2
                pe.wait_ge(f_xe[r], t + 1)
                if k >= 2:
                    pe.wait_ge(f_l, k - 1)
                for e in range(4):
                    last = nc.tensor.transpose(PS[:, k % 2, e * P:(e + 1) * P], XE[r][:, 4 * q + e, :], ID[:, :])
                last.then_inc(f_t, 1)

            def first(r, bank, signal):
                n = 0
                for e in range(E):
                    for x, w in ((XH, WH), (XH, WL), (XL, WH)):
                        last = mm(PS[:, bank, :], x[r][:, e * P:(e + 1) * P], w[:, r, e * I:(e + 1) * I],
                                  start=n == 0, stop=n == 3 * E - 1)
                        n += 1
                last.then_inc(signal, 1)

            pe.wait_ge(w_lo, NCH)
            pe.wait_ge(d_cgu, 2)
            for k in range(4):
                turn(k)
            for t in range(B + 1):
                if t < B:
                    pe.wait_ge(f_l, 4 * t + 2)
                    if t:
                        pe.wait_ge(f_int, t)
                    first(0, 2, f_g)
                if t + 1 < B:
                    turn(4 * t + 4)
                    turn(4 * t + 5)
                if t:
                    pe.wait_ge(f_itl, t)
                    pe.wait_ge(c_dve, 6)
                    if t >= 2:
                        pe.wait_ge(f_lg, t - 1)
                    n = 0
                    for c in range(IC):
                        for x, w in ((ITH, RDH), (ITH, RDL), (ITL, RDH)):
                            last = mm(PS[:, 7, 0:E], x[:, c * P:(c + 1) * P], w[:, c * E:(c + 1) * E],
                                      start=n == 0, stop=n == 3 * IC - 1)
                            n += 1
                    last.then_inc(f_ld, 1)
                if t < B:
                    pe.wait_ge(f_l, 4 * t + 4)
                    first(1, 3, f_u)
                if t + 1 < B:
                    turn(4 * t + 6)
                    turn(4 * t + 7)
                if t:
                    if t >= 2:
                        pe.wait_ge(f_acc, t - 1)
                    for half in range(2):
                        n = 0
                        for c in range(IC):
                            for x, w in ((ITH, WH), (ITH, WL), (ITL, WH)):
                                o = c * E * P + half * 512
                                last = mm(PS[:, 4 + half, :], x[:, c * P:(c + 1) * P], w[:, 2, o:o + 512],
                                          start=n == 0, stop=n == 3 * IC - 1)
                                n += 1
                    last.then_inc(f_dn, 1)
                if t < B:
                    pe.wait_ge(f_int, t + 1)
                    if t:
                        pe.wait_ge(f_itl, t)
                    for c in range(IC):
                        last = nc.tensor.transpose(PS[:, 6, c * P:(c + 1) * P], INT[:, c * P:(c + 1) * P], ID[:, :])
                    last.then_inc(f_it, 1)

        @block.vector
        def _(dve):
            v = nc.vector
            nd = [0]

            def step(ins):
                nd[0] += 1
                ins.then_inc(dv, 1)
                return nd[0]

            def link(ins):
                dve.wait_ge(dv, step(ins))

            for h in range(2):
                if h == 0:
                    dve.wait_ge(ld_x, NLX)
                    dve.wait_ge(c_id, 1)
                else:
                    dve.wait_ge(a_tc, h)
                for k in range(TAPS):
                    xs = XT[:, HB * h:HB * h + HB, k:k + P]
                    wk = CO[:, C_CW + k:C_CW + k + 1]
                    if k == 0:
                        link(v.tensor_scalar(ACC[:, :, :], xs, wk, None, ALU.mult))
                    elif k < TAPS - 1:
                        link(v.scalar_tensor_tensor(ACC[:, :, :], xs, wk, ACC[:, :, :], ALU.mult, ALU.add))
                    else:
                        v.scalar_tensor_tensor(ACC[:, :, :], xs, wk, ACC[:, :, :], ALU.mult, ALU.add)\
                            .then_inc(d_cand, 1)
                if h == 0:
                    dve.wait_ge(ld_q, 32)
                    dve.wait_ge(ld_k, NLK)
                    dve.wait_ge(ld_t, NLT)
                    wqf = flat(WQ[:, :, :])
                    v.tensor_scalar(wqf, wqf, SCALE, None, ALU.mult).then_inc(c_dve, 1)
                    step(v.tensor_scalar(BQ[:, :], CO[:, C_BQ:C_BQ + NG], SCALE, CO[:, C_QONE:C_QONE + 1],
                                         ALU.mult, ALU.add))
                    link(v.tensor_scalar(BK[:, :], CO[:, C_BK:C_BK + NG], CO[:, C_KONE:C_KONE + 1], None, ALU.add))
                    v.tensor_scalar(BQL[:, :], BQ[:, :], CO[:, C_QLOW:C_QLOW + 1], None, ALU.mult).then_inc(c_dve, 1)
                    v.tensor_scalar(BKL[:, :], BK[:, :], CO[:, C_KLOW:C_KLOW + 1], None, ALU.mult).then_inc(c_dve, 1)
                    v.memset(NM[:, :, :], 0.0).then_inc(c_dve, 1)
                    v.tensor_copy(RDH[:, :], RD[:, :]).then_inc(c_dve, 1)
                    dve.wait_ge(c_dve, 5)
                    v.tensor_tensor(RDL[:, :], RD[:, :], RDH[:, :].bitcast(F32), ALU.subtract).then_inc(c_dve, 1)

                def stack(j, S, bias, g):
                    dve.wait_ge(a_low, j + 1)
                    v.scalar_tensor_tensor(S[:, g, :], PS[:, 4 + j % 2, :], bias, LOW[:, j % 2, :].bitcast(F32),
                                           ALU.add, ALU.subtract).then_inc(d_st, 1)

                for g in range(NG):
                    stack(8 * h + g, KS, BK[:, g:g + 1], g)
                dve.wait_ge(pe_v, h + 1)
                if h:
                    dve.wait_ge(p_vm, HB * h)
                v.tensor_tensor(VB[:, :, :], PS[:, 7, :].rearrange("p (b t) -> p b t", b=HB),
                                RO[:, None, R_BV:R_BV + P].broadcast_to([P, HB, P]), ALU.add).then_inc(d_vb, 1)
                dve.wait_ge(a_tg, h + 1)
                dve.wait_ge(a_tc, h + 1)
                dve.wait_ge(c_act, 1)
                link(v.scalar_tensor_tensor(TG[:, :], TG[:, :], 1.0, TC[:, :], ALU.add, ALU.mult))
                for i in range(HB):
                    v.tensor_tensor_scan(HT[:, i * P:(i + 1) * P], DEC[:, :].broadcast_to([P, P]),
                                         TG[:, i * P:(i + 1) * P], 0.0, ALU.mult, ALU.add).then_inc(d_ht, 1)
                dve.wait_ge(pe_o, h + 1)
                dve.wait_ge(p_xb, h + 1)
                v.scalar_tensor_tensor(Y[:, :], PS[:, 7, :], 0.5, XB[:, :], ALU.mult, ALU.add).then_inc(d_y, 1)
                dve.wait_ge(p_rs, h + 1)
                for i in range(HB):
                    c = step(v.scalar_tensor_tensor(Y[:, i * P:(i + 1) * P], Y[:, i * P:(i + 1) * P], RS[:, i:i + 1],
                                                    RO[:, R_NW:R_NW + P], ALU.mult, ALU.mult))
                dve.wait_ge(dv, c)
                link(v.tensor_tensor(Y[:, :], Y[:, :], flat(X[:, HB * h:HB * h + HB, :]), ALU.add))

                def norm_stats(src, i):
                    link(v.bn_stats(ST6[:, i, :], src))
                    return v.bn_aggr(MV[:, i, :], ST6[:, i, :])

                for i in range(HB):
                    m = norm_stats(Y[:, i * P:(i + 1) * P], i)
                    if i < HB - 1:
                        step(m)
                m.then_inc(d_mv, 1)
                dve.wait_ge(d_mv, h + 1)
                dve.wait_ge(p_r1, h + 1)
                for i in range(HB):
                    v.tensor_scalar(X1[:, i * P:(i + 1) * P], Y[:, i * P:(i + 1) * P], MV[:, i, 0:1],
                                    RSTD[:, i:i + 1], ALU.subtract, ALU.mult).then_inc(d_x1, 1)
                for g in range(NG):
                    stack(8 * h + 4 + g, QS, BQ[:, g:g + 1], g)

                def maxima(i):
                    t = HB * h + i
                    for p in range(2):
                        dve.wait_ge(pe_s, 2 * t + p + 1)
                        v.tensor_reduce(NM[:, 2 * p:2 * p + 2, :], PS[:, 2 * p:2 * p + 2, :]
                                        .rearrange("q s (g k) -> q s g k", g=NG), AX_X, ALU.max, negate=True)\
                            .then_inc(d_max, 1)
                    dve.wait_ge(d_max, 2 * t + 2)
                    nm = NMS[:, :, :].rearrange("q g (s r) -> q s g r", s=NS)
                    if t:
                        dve.wait_ge(pe_aug, t)
                    link(v.tensor_copy(nm[:, :, :, MAX_HI].bitcast(F32R), NM[:, :, :]))
                    v.tensor_tensor(nm[:, :, :, MAX_LO], NM[:, :, :], nm[:, :, :, MAX_HI], ALU.subtract)\
                        .then_inc(d_nms, 1)

                def with_max(i):
                    t = HB * h + i
                    dve.wait_ge(pe_aug, t + 1)
                    if t:
                        dve.wait_ge(pe_st, 2 * t)
                    v.tensor_tensor(QSA[:, :, :], PS[:, 6, :].rearrange("r (g q) -> r g q", g=NG),
                                    QS[:, :, i * P:(i + 1) * P].bitcast(F32), ALU.add).then_inc(d_qsa, 1)

                def normalise(i):
                    t = HB * h + i
                    dve.wait_ge(pe_pv, t + 1)
                    link(v.reciprocal(RC[:, :], PS[:, 7, P:2 * P]))
                    if t:
                        dve.wait_ge(pe_wo, t)
                    v.tensor_tensor(OT[:, :], PS[:, 7, 0:P], RC[:, :], ALU.mult).then_inc(d_ot, 1)

                def residual(i):
                    t = HB * h + i
                    dve.wait_ge(pe_wo, t + 1)
                    dve.wait_ge(p_x1b, h + 1)
                    v.tensor_tensor(Z[:, i * P:(i + 1) * P], PS[:, 7, 2 * P:3 * P], X1B[:, i * P:(i + 1) * P], ALU.add)\
                        .then_inc(d_z, 1)
                    dve.wait_ge(d_z, t + 1)
                    m = norm_stats(Z[:, i * P:(i + 1) * P], i)
                    if i < HB - 1:
                        step(m)
                    else:
                        m.then_inc(d_mv2, 1)

                maxima(0)
                for i in range(HB + 1):
                    if i < HB:
                        with_max(i)
                    if i:
                        normalise(i - 1)
                        residual(i - 1)
                    if i + 1 < HB:
                        maxima(i + 1)
                dve.wait_ge(d_mv2, h + 1)
                dve.wait_ge(p_r2, h + 1)
                for i in range(HB):
                    v.tensor_scalar(X2[:, HB * h + i, :], Z[:, i * P:(i + 1) * P], MV[:, i, 0:1],
                                    RSTD[:, i:i + 1], ALU.subtract, ALU.mult).then_inc(d_x2, 1)
                dve.wait_ge(pe_lg, h + 1)
                link(v.tensor_copy(LG[:, :, :], PS[:, 7, 0:2 * E * HB].rearrange("p (a e) -> p a e", e=E)))
                for a in range(2 * HB):
                    c = step(v.max(V8[:, a, :], LG[:, a, :]))
                dve.wait_ge(dv, c)
                for a in range(2 * HB):
                    c = step(v.max_index(I8[:, a, :], V8[:, a, :], LG[:, a, :]))
                if h:
                    dve.wait_ge(a_ex, h)
                v.tensor_tensor(DV[:, :], V8[:, :, 1], V8[:, :, 0], ALU.subtract).then_inc(d_dv, 1)
                dve.wait_ge(dv, c)
                link(v.tensor_copy(IF[:, :, :], I8[:, :, 0:2]))
                dve.wait_ge(a_ex, h + 1)
                link(v.tensor_scalar(SM[:, :], EX[:, :], 1.0, None, ALU.add))
                link(v.reciprocal(P0[:, :], SM[:, :]))
                step(v.tensor_tensor(P1[:, :], EX[:, :], P0[:, :], ALU.mult))
                iota = RO[:, None, R_IO:R_IO + E].broadcast_to([P, 2 * HB, E])
                cg = CGU[:, HB * h:HB * h + HB, :, :].rearrange("p b r e -> p (b r) e")

                def wide(ap):
                    return ap.broadcast_to([P, 2 * HB, E])

                link(v.tensor_tensor(cg, iota, wide(IF[:, :, 0:1]), ALU.is_equal))
                step(v.tensor_tensor(cg, cg, wide(P0[:, :, None]), ALU.mult))
                link(v.tensor_tensor(OH[:, :, :], iota, wide(IF[:, :, 1:2]), ALU.is_equal))
                link(v.tensor_tensor(OH[:, :, :], OH[:, :, :], wide(P1[:, :, None]), ALU.mult))
                v.tensor_tensor(cg, cg, OH[:, :, :], ALU.add).then_inc(d_cgu, 1)

            def low(k):
                r, q = k // 2 % 2, k % 2
                dve.wait_ge(f_h, k + 1)
                c = slice(q * 512, q * 512 + 512)
                v.tensor_tensor(XL[r][:, c], PS[:, k % 2, :], XH[r][:, c].bitcast(F32), ALU.subtract).then_inc(f_l, 1)

            for k in range(4):
                low(k)
            for t in range(B + 1):
                if t + 1 < B:
                    low(4 * t + 4)
                    low(4 * t + 5)
                if t:
                    dve.wait_ge(f_ld, t)
                    v.tensor_copy(DLG[:, :], PS[:, 7, 0:E]).then_inc(f_lg, 1)
                    dve.wait_ge(f_lg, t)
                    link(v.max(DV8[:, :], DLG[:, :]))
                    v.tensor_tensor(DD[:, :], DV8[:, 1:2], DV8[:, 0:1], ALU.subtract).then_inc(f_dd, 1)
                    link(v.max_index(DI8[:, :], DV8[:, :], DLG[:, :]))
                    step(v.tensor_copy(DIF[:, :], DI8[:, 0:2]))
                    dve.wait_ge(f_de, t)
                    link(v.tensor_scalar(DS[:, :], DE[:, :], 1.0, None, ALU.add))
                    link(v.reciprocal(DP[:, 0:1], DS[:, :]))
                    link(v.tensor_tensor(DP[:, 1:2], DE[:, :], DP[:, 0:1], ALU.mult))
                    for j in range(2):
                        c = step(v.tensor_scalar(DC[:, j, :], RO[:, R_IO:R_IO + E], DIF[:, j:j + 1], DP[:, j:j + 1],
                                                 ALU.is_equal, ALU.mult))
                    dve.wait_ge(dv, c)
                    link(v.tensor_tensor(CD[:, :], DC[:, 0, :], DC[:, 1, :], ALU.add))
                if t < B:
                    dve.wait_ge(f_th, t + 1)
                    link(v.scalar_tensor_tensor(SG[:, :], TH[:, :], 1.0, PS[:, 2, :], ALU.add, ALU.mult))
                    dve.wait_ge(f_u, t + 1)
                    if t:
                        dve.wait_ge(f_it, t)
                    v.scalar_tensor_tensor(INT[:, :], SG[:, :], 0.5, PS[:, 3, :], ALU.mult, ALU.mult)\
                        .then_inc(f_int, 1)
                if t + 1 < B:
                    low(4 * t + 6)
                    low(4 * t + 7)
                if t < B:
                    dve.wait_ge(f_ith, t + 1)
                    v.tensor_tensor(ITL[:, :], PS[:, 6, :], ITH[:, :].bitcast(F32), ALU.subtract).then_inc(f_itl, 1)
                if t:
                    dve.wait_ge(f_dn, t)
                    for e in range(E):
                        src = X2[:, t - 1, :] if e == 0 else YD[:, (e - 1) % 2, :]
                        ins = v.scalar_tensor_tensor(YD[:, e % 2, :], PS[:, 4 + e // 4, (e % 4) * P:(e % 4 + 1) * P],
                                                     CD[:, e:e + 1], src, ALU.mult, ALU.add)
                        if e < E - 1:
                            link(ins)
                        else:
                            ins.then_inc(f_acc, 1)
                    dve.wait_ge(f_acc, t)
                    y = YD[:, (E - 1) % 2, :]
                    link(v.bn_stats(S6[:, :], y))
                    v.bn_aggr(M2[:, :], S6[:, :]).then_inc(f_mv, 1)
                    dve.wait_ge(f_mv, t)
                    dve.wait_ge(f_r, t)
                    if t >= 3:
                        dve.wait_ge(st[(t - 1) % 2], 16 * ((t - 1) // 2))
                    v.tensor_scalar(OUT[:, (t - 1) % 2, :], y, M2[:, 0:1], R1[:, :], ALU.subtract, ALU.mult)\
                        .then_inc(f_out, 1)


def kernel(**inputs):
    import numpy as np
    import concourse.bacc as bacc
    from concourse.bass_utils import run_bass_kernel_spmd

    a = {k: np.asarray(v) for k, v in inputs.items()}

    def c(v):
        return np.ascontiguousarray(v)

    r = np.arange(P)
    slot, row = r // 32, r % 32
    used = row < 3 * DH

    def stacked(w):
        g = np.arange(NG)[:, None]
        idx = (NS * g + slot[None, :]) * DH + (row % DH)[None, :]
        return np.where(used, w[..., idx], np.float32(0))

    def marks(*which):
        return np.isin(row, which).astype(np.float32)[:, None]

    cols = np.concatenate([
        a["L0_attn_gate_w"][:, 0, :], a["L0_attn_cand_w"][:, 0, :],
        a["L0_attn_gate_b"][:, None], a["L0_attn_cand_b"][:, None], a["L0_attn_log_decay"][:, None],
        stacked(a["L0_xattn_bq"]).T, stacked(a["L0_xattn_bk"]).T,
        marks(MASK_HI, MASK_LO), marks(MAX_HI, MAX_LO),
        marks(*range(LO_HI, LO_HI + DH)), marks(*range(HI_LO, HI_LO + DH), MASK_LO)], axis=1)
    head_mask = (r[None, :] % 32 // DH == np.arange(NS)[:, None]).astype(np.float32)
    rows = np.concatenate([
        a["L0_attn_out_b"], a["L0_attn_norm_w"], a["L0_xattn_bv"], a["L0_xattn_bp"],
        head_mask.reshape(-1), np.arange(E, dtype=np.float32)])
    arrays = {
        "x_tok": c(a["x"].transpose(1, 0, 2)),
        "x_t": c(a["x"].transpose(2, 0, 1)),
        "ctx_t": c(a["ctx_1024"].transpose(2, 0, 1).reshape(P, B * P)),
        "mask": c(a["mask_BxS2_ff0"].reshape(1, B * P)),
        "cols": c(cols),
        "rows": c(rows),
        "out_w": c(a["L0_attn_out_w"].T),
        "w_q": c(stacked(a["L0_xattn_Wq"])),
        "w_k": c(stacked(a["L0_xattn_Wk"])),
        "w_v": c(a["L0_xattn_Wv"]),
        "w_p": c(a["L0_xattn_Wp"]),
        "mask_rows": c(marks(MASK_HI, MASK_LO).T),
        "r_gu": c(np.concatenate([a["L0_ffn_router_gate"], a["L0_ffn_router_up"]]).T),
        "r_down": c(a["L0_ffn_router_down"].reshape(E, IC, P).transpose(2, 1, 0).reshape(P, IC * E)),
        "w_gate": c(a["L0_ffn_w_gate"].transpose(2, 0, 1).reshape(P, E * I)),
        "w_up": c(a["L0_ffn_w_up"].transpose(2, 0, 1).reshape(P, E * I)),
        "w_down": c(a["L0_ffn_w_down"].reshape(E, P, IC, P).transpose(3, 2, 0, 1).reshape(P, IC * E * P)),
    }
    nc = bacc.Bacc("TRN2", target_bir_lowering=False, num_devices=1)
    args = [nc.dram_tensor(n, v.shape, mybir.dt.from_np(v.dtype), kind="ExternalInput").ap() for n, v in arrays.items()]
    out = nc.dram_tensor("y_out", (B, P, P), F32, kind="ExternalOutput").ap()
    decoder_layer(nc, *args, out)
    result = run_bass_kernel_spmd(nc, [arrays], core_ids=[0])
    return result.results[0]["y_out"]
```

```python
from contextlib import ExitStack

import concourse.bass as bass
from concourse import mybir

F32 = mybir.dt.float32
F32R = mybir.dt.float32r
BF16 = mybir.dt.bfloat16
U32 = mybir.dt.uint32
ALU = mybir.AluOpType
ACT = mybir.ActivationFunctionType
AX_X = mybir.AxisListType.X

P = 128
B = 8
HB = 4
TAPS = 7
PAD = TAPS // 2
ROW = P + 2 * PAD
HEADS, DH = 16, 8
NG = 4
NS = 4
E = 8
I = 512
IC = I // P
SCALE = float(DH) ** -0.5
RMS_EPS = 1.1920929e-07
LN_EPS = 1e-05
WCH = 1024
NCH = 3 * E * I // WCH
CPW = E * I // WCH
CAUSAL = -3.3895313892515355e38

C_GW, C_CW, C_GB, C_CB, C_LD = 0, TAPS, 2 * TAPS, 2 * TAPS + 1, 2 * TAPS + 2
C_QLOW = C_LD + 1
C_KLOW = C_QLOW + 1
C_AS = C_KLOW + 1
C_AW = C_AS + 1
C_AM = C_AW + 1
NCOL = C_AM + 1
A_ROWS, A_QROWS = 5, 3
A_K, A_Q, A_T = 0, NG * P, 2 * NG * P
A_COLS = 2 * NG * P + B * P
R_OB, R_NW, R_BV, R_BP, R_HM, R_IO = 0, P, 2 * P, 3 * P, 4 * P, 4 * P + NS * P
NROW = R_IO + E
HI_HI, HI_LO, LO_HI, MASK_HI, MASK_LO, MAX_HI, MAX_LO = 0, DH, 2 * DH, 3 * DH, 3 * DH + 1, 3 * DH + 2, 3 * DH + 3



def before_tiles():
    taps = iter(range(2 * TAPS))

    def fill(n):
        yield from (("C1", k) for _, k in zip(range(n), taps))

    yield from (("GC",), ("W", 0), ("W", 1), ("GT", 0), ("AX",), ("RD",), ("O", 0), ("K", 0), ("KE", 0))
    yield from (("W", 2), ("W", 3))
    yield from fill(7)
    yield from (("N1", 0), ("X1", 0), ("W", 4), ("W", 5), ("DC",))
    yield from (("V", 0), ("Q", 0), ("VM", 0), ("QE", 0))
    yield from fill(3)
    yield from (("S", 0, 0), ("S", 0, 1), ("NM", 0), ("W", 6))
    yield from fill(2)
    yield from tile_zero(fill)


def tile_zero(fill):
    for at, step in tile_plan(0):
        yield step
        if step[0] == "K":
            yield from fill(1)
        elif step == ("ST", 0, 1):
            yield ("W", 7)
            yield ("W", 8)
            yield from fill(1)
        elif step == ("PV", 0, 1):
            yield ("W", 9)
            yield ("W", 10)
        elif step == ("N2", 0):
            yield ("W", 11)


def tile_plan(t):
    steps = [(0, ("V", t + 1)), (0.5, ("A", t)), (1, ("K", t + 1)), (2, ("Q", t + 1)), (2, ("KE", t + 1)),
             (2, ("QE", t + 1)), (5, ("VM", t + 1)), (5, ("ST", t, 0)), (6.5, ("ST", t, 1)),
             (8.5, ("PV", t, 0)), (10, ("PV", t, 1)), (11, ("S", t + 1, 0)), (12.5, ("WO", t)),
             (13, ("S", t + 1, 1)), (14, ("N2", t)), (15, ("NM", t + 1)), (16.5, ("X2", t)), (17.5, ("LG", t)),
             (20.5, ("XE", 4 * t)), (20.5, ("XE", 4 * t + 1))]
    return [(at, step) for at, step in steps if step[0] == "XE" or step[1] < B]


def expert_plan(t):
    following = t + 1 < B
    if t < B:
        for e in range(E):
            yield ("G", t, e)
            if t >= 2 and e == 2:
                yield ("F", t - 2)
            if t and e == 4:
                yield ("L", t - 1)
        for e in range(E):
            yield ("U", t, e)
            if t and e == 1:
                yield ("LL", t - 1)
            if e in (2, 5) and following:
                yield ("T", 4 * t + 4 + e // 3)
    else:
        yield ("F", t - 2)
        yield ("L", t - 1)
        yield ("LL", t - 1)
    if t == 0:
        yield ("T", 6)
        yield ("T", 7)
    else:
        for half in range(2):
            for c in range(IC):
                yield ("D", t - 1, half, c)
                if half == 0 and c in (0, 3) and following:
                    yield ("T", 4 * t + 6 + c // 3)
    if t < B:
        yield ("IT", t)
    else:
        yield ("F", t - 1)


def schedule():
    per_tile = 3 * E
    attention = []
    for t in range(1, B):
        start = {1: -LEAD, 2: SECOND}.get(t, per_tile * (t - 2))
        end = SECOND if t == 1 else per_tile * (t - 1)
        attention += [(start + (end - start) * at / per_tile, step) for at, step in tile_plan(t)]
    attention += [(1, ("GT", 1)), (5, ("O", 1)), (7, ("N1", 1)), (15, ("X1", 1))]
    attention.sort(key=lambda x: x[0])
    plan = list(before_tiles())
    now = 0
    for k in range(4):
        plan.append(("T", k))
        if k < 2:
            plan.append(("XE", k + 2))
    for t in range(B + 1):
        for step in expert_plan(t):
            if step[0] in "GUD":
                while attention and attention[0][0] <= now:
                    plan.append(attention.pop(0)[1])
                now += 1
            plan.append(step)
            if step[0] == "T" and step[1] % 4 < 2:
                plan.append(("XE", step[1] + 2))
    return plan


LEAD, SECOND = 12, 4


def decoder_layer(nc, x_tok, x_t, ctx_t, cols, rows, aux, out_w, w_q, w_k, w_v, w_p,
                  r_gu, r_down, w_gate, w_up, w_down, out):
    with ExitStack() as ctx:
        def sb(name, shape, dt=F32):
            return ctx.enter_context(nc.sbuf_tensor(name, shape, dt))

        def sem(name):
            return ctx.enter_context(nc.semaphore(name))

        XT = sb("XT", [P, B, ROW])
        X = sb("X", [P, B, P])
        CT = sb("CT", [P, B * P])
        AUX = sb("AUX", [A_ROWS, A_COLS], F32R)
        CO = sb("CO", [P, NCOL])
        RO = sb("RO", [P, NROW])
        OW = sb("OW", [P, P])
        WQ = sb("WQ", [P, NG, P])
        WK = sb("WK", [P, NG, P])
        WV = sb("WV", [P, P])
        WP = sb("WP", [P, P])
        RGU = sb("RGU", [P, 2 * E])
        RD = sb("RD", [P, IC * E])
        RDH = sb("RDH", [P, IC * E], F32R)
        RDL = sb("RDL", [P, IC * E], F32R)
        ID = sb("ID", [P, P])
        IDB = sb("IDB", [P, P], BF16)
        CM = sb("CM", [P, P], BF16)
        DIAG = sb("DIAG", [P, TAPS, P])
        DEC = sb("DEC", [P, 1])
        HGB = sb("HGB", [P, 1])
        MHALF = sb("MHALF", [P, HB])
        WH = sb("WH", [P, 3, E * I], F32R)
        WL = sb("WL", [P, 3, E * I], F32R)
        CAND = sb("CAND", [P, HB * P])
        GATE = sb("GATE", [P, HB * P])
        Y = sb("Y", [P, B, P])
        MS = sb("MS", [P, B])
        RS = sb("RS", [P, B])
        ST6 = sb("ST6", [P, HB, 6])
        MV = sb("MV", [P, B, 2])
        RSTD = sb("RSTD", [P, B])
        X1T = sb("X1T", [P, B * P])
        LOW = sb("LOW", [P, 2, NG * P], F32R)
        QS = sb("QS", [P, 2, NG, P], F32R)
        KS = sb("KS", [P, 2, NG, P], F32R)
        QSA = sb("QSA", [P, NG, P], F32R)
        VB = sb("VB", [P, 2, P])
        VM = sb("VM", [P, 2, NS, P])
        NM = sb("NM", [P, NS, NG])
        NMS = sb("NMS", [P, NG, P])
        PT = sb("PT", [P, NS, NG, P])
        RC = sb("RC", [P, P])
        OT = sb("OT", [P, P])
        ZST = sb("ZST", [P, 6])
        ZMV = sb("ZMV", [P, 2])
        ZR = sb("ZR", [P, 1])
        X2T = sb("X2T", [P, P])
        LG = sb("LG", [P, 2, E])
        V8 = sb("V8", [P, 2, 8])
        I8 = sb("I8", [P, 2, 8], U32)
        IF = sb("IF", [P, 2, 2])
        DV = sb("DV", [P, 2])
        EX = sb("EX", [P, 2])
        SM = sb("SM", [P, 2])
        P0 = sb("P0", [P, 2])
        P1 = sb("P1", [P, 2])
        OH = sb("OH", [P, 2, E])
        CGU = sb("CGU", [P, B, 2, E])
        XH = sb("XH", [P, 2, E * P], F32R)
        XL = sb("XL", [P, 2, E * P], F32R)
        ITH = sb("ITH", [P, I], F32R)
        ITL = sb("ITL", [P, I], F32R)
        LT = sb("LT", [E, P])
        DLG = sb("DLG", [P, E])
        DV8 = sb("DV8", [P, 8])
        DI8 = sb("DI8", [P, 8], U32)
        DIF = sb("DIF", [P, 2])
        DD = sb("DD", [P, 1])
        DE = sb("DE", [P, 1])
        DS = sb("DS", [P, 1])
        DP = sb("DP", [P, 2])
        DC = sb("DC", [P, 2, E])
        CD = sb("CD", [P, E])
        S6 = sb("S6", [P, 6])
        M2 = sb("M2", [P, 2])
        R1 = sb("R1", [P, 1])
        ROOM = sb("ROOM", [P, 2 * WCH])
        RAW = ROOM[:, :].rearrange("p (s c) -> p s c", s=2)
        XE = ROOM[:, 0:1024].rearrange("p (s e t) -> p s e t", s=2, e=4)
        TH = sb("TH", [P, I])
        INT = ROOM[:, 1024:1536]
        YD = ROOM[:, 1536:1792].rearrange("p (s t) -> p s t", s=2)
        OUT = ROOM[:, 1792:2048].rearrange("p (s t) -> p s t", s=2)

        PS = ctx.enter_context(nc.psum_tensor("PS", [P, 8, 512], F32))
        B_GC, B_CC, B_O = [0, 2], 3, [1, 3]
        PAIRS, LATER = [5, 0], 5
        FIRST_JOBS = 7
        ONE = 7
        TURN, LOGIT = 0, 4

        AUX_RAW = PT[0:A_ROWS, :, :, :].rearrange("p a b c -> p (a b c)")
        AUX_LOW = XH[0:A_ROWS, :, :].rearrange("p a b -> p (a b)")

        ld_x = sem("ld_x")
        ld_k = sem("ld_k")
        ld_t = sem("ld_t")
        ld_q = sem("ld_q")
        ld_w = [sem("ld_w0"), sem("ld_w1")]
        c_id = sem("c_id")
        c_dg = sem("c_dg")
        c_dve = sem("c_dve")
        c_act = sem("c_act")
        c_dgc = sem("c_dgc")
        c_aux = sem("c_aux")
        dv = sem("dv")
        pl = sem("pl")
        w_hi = [sem("w_hi0"), sem("w_hi1")]
        w_lo = [sem("w_lo0"), sem("w_lo1")]
        pe_gc = sem("pe_gc"); pe_cc = sem("pe_cc"); pe_p = sem("pe_p"); pe_v = sem("pe_v"); pe_o = sem("pe_o")
        pe_x1 = sem("pe_x1"); pe_s = sem("pe_s"); pe_aug = sem("pe_aug"); pe_st = sem("pe_st")
        pe_pv = sem("pe_pv"); pe_wo = sem("pe_wo"); pe_x2 = sem("pe_x2"); pe_lg = sem("pe_lg")
        a_tg = sem("a_tg"); a_tc = sem("a_tc"); a_low = sem("a_low"); a_ms = sem("a_ms")
        a_x1 = sem("a_x1"); a_exp = sem("a_exp"); a_x2 = sem("a_x2"); a_ex = sem("a_ex")
        d_cand = sem("d_cand"); d_vb = sem("d_vb"); d_st = sem("d_st"); d_ht = sem("d_ht")
        d_y = sem("d_y"); d_mv = sem("d_mv"); d_x1 = sem("d_x1"); d_max = sem("d_max")
        d_nms = sem("d_nms"); d_qsa = sem("d_qsa"); d_ot = sem("d_ot"); d_z = sem("d_z")
        d_mv2 = sem("d_mv2"); d_x2 = sem("d_x2"); d_dv = sem("d_dv"); d_cgu = sem("d_cgu")
        d_lg = sem("d_lg")
        p_xb = sem("p_xb"); p_rs = sem("p_rs"); p_r1 = sem("p_r1"); p_x1b = sem("p_x1b")
        p_vm = sem("p_vm"); p_sel = sem("p_sel"); p_r2 = sem("p_r2")
        f_xe = sem("f_xe"); f_t = sem("f_t"); f_h = sem("f_h"); f_l = sem("f_l")
        f_g = sem("f_g"); f_u = sem("f_u"); f_th = sem("f_th"); f_sg = sem("f_sg"); f_int = sem("f_int")
        f_it = sem("f_it"); f_ith = sem("f_ith"); f_itl = sem("f_itl"); f_ld = sem("f_ld")
        f_lt = sem("f_lt"); f_ll = sem("f_ll"); f_dd = sem("f_dd"); f_de = sem("f_de"); f_lg = sem("f_lg")
        f_d0 = sem("f_d0"); f_d1 = sem("f_d1"); f_a0 = sem("f_a0"); f_acc = sem("f_acc")
        f_mv = sem("f_mv"); f_r = sem("f_r"); f_out = sem("f_out")
        st = [sem("st0"), sem("st1")]

        block = ctx.enter_context(nc.Block())
        NLX, NLK, NLT = 2 * 16, 5 * 16, 4 * 16

        def flat(ap):
            return ap.rearrange("p a b -> p (a b)")

        def product_bank(t, which):
            return 1 + (4 * t + which) % 3

        plan = schedule()
        jobs = [x for x in plan if x[0] in ("K", "S", "ST")]

        def pair_bank(*job):
            n = jobs.index(job)
            return PAIRS[n % 2] if n < FIRST_JOBS else LATER

        def job_before(*job):
            n = jobs.index(job)
            same = [j for j in jobs[:n] if pair_bank(*j) == pair_bank(*job)]
            return same[-1] if same else None

        w_src = [w_gate, w_up, w_down]

        def chunk(c):
            return c // CPW, (c % CPW) * WCH

        def split_by_dve(c):
            return c % 4 == 3

        @block.sync
        def _(sp):
            sp.dma_start(XT[:, :, PAD:PAD + P], x_t).then_inc(ld_x, 16)
            sp.dma_start(CO[:, :], cols).then_inc(ld_x, 16)
            sp.dma_start(CT[:, :], ctx_t).then_inc(ld_k, 16)
            sp.dma_start(WK[:, :, :], w_k).then_inc(ld_k, 16)
            sp.dma_start(AUX_RAW, aux).then_inc(ld_k, 16)
            sp.dma_start(WV[:, :], w_v).then_inc(ld_k, 16)
            sp.dma_start(RO[:, :], rows.partition_broadcast(P)).then_inc(ld_k, 16)
            for c in range(NCH):
                if c >= 2:
                    sp.wait_ge(w_lo[c % 2], c // 2)
                w, o = chunk(c)
                sp.dma_start(RAW[:, c % 2, :], w_src[w][:, o:o + WCH]).then_inc(ld_w[c % 2], 16)
            for t in range(B):
                sp.wait_ge(f_out, t + 1)
                sp.dma_start(out[t], OUT[:, t % 2, :]).then_inc(st[t % 2], 16)
            for q in st:
                sp.wait_ge(q, 16 * B // 2)

        @block.gpsimd
        def _(pool):
            g = nc.gpsimd
            np_ = [0]

            def step(ins):
                np_[0] += 1
                ins.then_inc(pl, 1)
                return np_[0]

            g.memset(XT[:, :, 0:PAD], 0.0)
            g.memset(XT[:, :, PAD + P:ROW], 0.0).then_inc(c_id, 1)
            step(g.memset(ID[:, :], 0.0))
            n = step(g.memset(CM[:, :], 0.0))
            pool.wait_ge(pl, n)
            g.affine_select(out=ID[:, :], in_=ID[:, :], compare_op=ALU.not_equal, fill=1.0, base=0,
                            pattern=[[-1, P]], channel_multiplier=1).then_inc(c_id, 1)
            g.affine_select(out=CM[:, :], in_=CM[:, :], compare_op=ALU.is_ge, fill=CAUSAL, base=0,
                            pattern=[[-1, P]], channel_multiplier=1).then_inc(c_id, 1)
            pool.wait_ge(c_id, 2)
            g.tensor_copy(IDB[:, :], ID[:, :]).then_inc(c_id, 1)
            g.memset(NMS[:, :, :], 0.0)
            g.memset(MHALF[:, :], -0.5).then_inc(c_id, 1)
            pool.wait_ge(c_id, 5)

            def inv_sqrt(dst, src, scale, eps, n):
                pool.wait_ge(pl, step(g.tensor_scalar(dst, src, scale, eps, ALU.mult, ALU.add)))
                return g.tensor_tensor(dst, dst, MHALF[:, 0:n], ALU.pow)

            pool.wait_ge(ld_k, NLK)
            pool.wait_ge(ld_t, NLT)
            g.tensor_tensor(Y[:, :, :], X[:, :, :], RO[:, None, R_OB:R_OB + P].broadcast_to([P, B, P]), ALU.add)\
                .then_inc(p_xb, 1)

            for x in plan:
                what, args = x[0], x[1:]
                if what == "W" and not split_by_dve(args[0]):
                    c, = args
                    w, o = chunk(c)
                    pool.wait_ge(w_hi[c % 2], c // 2 + 1)
                    g.tensor_tensor(WL[:, w, o:o + WCH], RAW[:, c % 2, :], WH[:, w, o:o + WCH].bitcast(F32),
                                    ALU.subtract).then_inc(w_lo[c % 2], 1)
                elif what == "N1":
                    h, = args
                    half = slice(HB * h, HB * h + HB)
                    pool.wait_ge(a_ms, HB * (h + 1))
                    inv_sqrt(RS[:, half], MS[:, half], 1.0 / P, RMS_EPS, HB).then_inc(p_rs, 1)
                    pool.wait_ge(d_mv, h + 1)
                    inv_sqrt(RSTD[:, half], MV[:, half, 1], 1.0, LN_EPS, HB).then_inc(p_r1, 1)
                elif what == "Q" and args[0] % HB == 0:
                    h = args[0] // HB
                    pool.wait_ge(pe_x1, h + 1)
                    half = Y[:, HB * h:HB * h + HB, :]
                    g.tensor_tensor(half, half, RO[:, None, R_BP:R_BP + P].broadcast_to([P, HB, P]), ALU.add)\
                        .then_inc(p_x1b, 1)
                elif what == "VM":
                    t, = args
                    pool.wait_ge(d_vb, t + 1)
                    if t >= 2:
                        pool.wait_ge(pe_pv, 2 * (t - 1))
                    g.tensor_tensor(VM[:, t % 2, :, :], VB[:, t % 2, None, :].broadcast_to([P, NS, P]),
                                    RO[:, R_HM:R_HM + NS * P].rearrange("p (s d) -> p s d", s=NS),
                                    ALU.mult).then_inc(p_vm, 1)
                elif what == "ST":
                    t, p = args
                    pool.wait_ge(a_exp, 2 * t + p + 1)
                    v = PT[:, 2 * p:2 * p + 2, :, :].rearrange("k s g q -> k (s g) q")
                    g.affine_select(out=v, in_=v, compare_op=ALU.is_ge, fill=0.0, base=0,
                                    pattern=[[0, 2 * NG], [1, P]], channel_multiplier=-1).then_inc(p_sel, 1)
                elif what == "N2":
                    t, = args
                    pool.wait_ge(d_mv2, t + 1)
                    inv_sqrt(ZR[:, :], ZMV[:, 1:2], 1.0, LN_EPS, 1).then_inc(p_r2, 1)
                elif what == "XE":
                    k, = args
                    t, r, q = k // 4, k // 2 % 2, k % 2
                    if k == 0:
                        pool.wait_ge(w_lo[0], NCH // 2)
                        pool.wait_ge(w_lo[1], NCH // 2)
                    if k >= 2:
                        pool.wait_ge(f_t, k - 1)
                    if k % 4 == 0:
                        pool.wait_ge(d_cgu, t + 1)
                    g.tensor_tensor(XE[:, k % 2, :, :], X[:, t, None, :].broadcast_to([P, 4, P]),
                                    CGU[:, t, r, 4 * q:4 * q + 4, None].broadcast_to([P, 4, P]), ALU.mult)\
                        .then_inc(f_xe, 1)
                elif what == "F":
                    pool.wait_ge(f_mv, args[0] + 1)
                    inv_sqrt(R1[:, :], M2[:, 1:2], 1.0, LN_EPS, 1).then_inc(f_r, 1)

        @block.scalar
        def _(act):
            s = nc.scalar
            act.dma_start(X[:, :, :], x_tok).then_inc(ld_t, 16)
            act.dma_start(OW[:, :], out_w).then_inc(ld_t, 16)
            act.dma_start(RGU[:, :], r_gu).then_inc(ld_t, 16)
            act.dma_start(RD[:, :], r_down).then_inc(ld_t, 16)
            act.dma_start(WQ[:, :, :], w_q).then_inc(ld_q, 16)
            act.dma_start(WP[:, :], w_p).then_inc(ld_q, 16)
            act.wait_ge(ld_x, NLX)
            s.activation(DEC[:, :], CO[:, C_LD:C_LD + 1], ACT.Exp).then_inc(c_act, 1)

            act.wait_ge(ld_k, NLK)
            aux_q = AUX_RAW[:, A_Q:A_T]
            s.activation(aux_q, aux_q, ACT.Copy, scale=CO[0:A_ROWS, C_AS:C_AS + 1]).then_inc(c_aux, 1)
            s.activation(AUX_LOW[:, A_T:A_COLS], AUX_RAW[:, A_T:A_COLS], ACT.Copy,
                         scale=CO[0:A_ROWS, C_AM:C_AM + 1]).then_inc(c_aux, 1)
            act.wait_ge(c_aux, 1)
            s.activation(AUX_LOW[:, 0:A_T], AUX_RAW[:, 0:A_T], ACT.Copy,
                         scale=CO[0:A_ROWS, C_AW:C_AW + 1]).then_inc(c_aux, 1)

            def low_rows(j, bank, low):
                act.wait_ge(pe_p, j + 1)
                if j >= 2:
                    act.wait_ge(d_st, j - 1)
                s.activation(LOW[:, j % 2, :], PS[:, bank, :], ACT.Copy, scale=low).then_inc(a_low, 1)

            for x in plan:
                what, args = x[0], x[1:]
                if what == "W":
                    c, = args
                    w, o = chunk(c)
                    act.wait_ge(ld_w[c % 2], 16 * (c // 2 + 1))
                    s.copy(WH[:, w, o:o + WCH], RAW[:, c % 2, :]).then_inc(w_hi[c % 2], 1)
                elif what == "DC":
                    act.wait_ge(pe_gc, 2)
                    for k in range(TAPS):
                        s.activation(DIAG[:, k, :], ID[:, :], ACT.Copy, scale=CO[:, C_CW + k:C_CW + k + 1])\
                            .then_inc(c_dgc, 1)
                elif what == "GT":
                    h, = args
                    if h == 0:
                        act.wait_ge(d_cand, 1)
                        cand = CAND[:, :]
                    else:
                        act.wait_ge(pe_cc, 1)
                        act.wait_ge(pe_o, 1)
                        act.wait_ge(a_ms, HB)
                        cand = PS[:, B_CC, :]
                    s.activation(CAND[:, :], cand, ACT.Tanh, bias=CO[:, C_CB:C_CB + 1]).then_inc(a_tc, 1)
                    act.wait_ge(pe_gc, h + 1)
                    act.wait_ge(c_dve, 1)
                    s.activation(GATE[:, :], PS[:, B_GC[h], :], ACT.Tanh, bias=HGB[:, :], scale=0.5)\
                        .then_inc(a_tg, 1)
                elif what == "KE":
                    t, = args
                    low_rows(2 * t, pair_bank("K", t), CO[:, C_KLOW:C_KLOW + 1])
                elif what == "QE":
                    t, = args
                    low_rows(2 * t + 1, pair_bank("K", t) + 1, CO[:, C_QLOW:C_QLOW + 1])
                elif what == "O":
                    h, = args
                    act.wait_ge(d_y, h + 1)
                    for i in range(HB * h, HB * h + HB):
                        if i:
                            act.wait_ge(a_ms, i)
                        s.activation(GATE[:, 0:P], Y[:, i, :], ACT.Square, accum_out=MS[:, i:i + 1]).then_inc(a_ms, 1)
                elif what == "X1":
                    h, = args
                    act.wait_ge(pe_x1, h + 1)
                    s.copy(X1T[:, HB * P * h:HB * P * (h + 1)], PS[:, B_O[h], :]).then_inc(a_x1, 1)
                elif what == "ST":
                    t, p = args
                    act.wait_ge(pe_st, 2 * t + p + 1)
                    if t:
                        act.wait_ge(pe_pv, 2 * t + p - 1)
                    b = pair_bank(*x)
                    s.activation(PT[:, 2 * p:2 * p + 2, :, :].rearrange("k s g q -> k (s g q)"),
                                 PS[:, b:b + 2, :].rearrange("k s c -> k (s c)"), ACT.Exp).then_inc(a_exp, 1)
                elif what == "X2":
                    t, = args
                    act.wait_ge(pe_x2, t + 1)
                    if t:
                        act.wait_ge(pe_lg, t)
                    s.copy(X2T[:, :], PS[:, ONE, 0:P]).then_inc(a_x2, 1)
                elif what == "LG":
                    t, = args
                    act.wait_ge(d_dv, t + 1)
                    s.activation(EX[:, :], DV[:, :], ACT.Exp).then_inc(a_ex, 1)
                elif what == "T":
                    k, = args
                    r, q = k // 2 % 2, k % 2
                    act.wait_ge(f_t, k + 1)
                    s.copy(XH[:, r, q * 512:q * 512 + 512], PS[:, TURN, :]).then_inc(f_h, 1)
                elif what == "G" and args[1] == E - 1:
                    t = args[0]
                    act.wait_ge(f_g, t + 1)
                    if t:
                        act.wait_ge(f_int, t)
                    s.activation(TH[:, :], PS[:, product_bank(t, 0), :], ACT.Tanh, scale=0.5).then_inc(f_th, 1)
                elif what == "IT":
                    t, = args
                    act.wait_ge(f_it, t + 1)
                    s.copy(ITH[:, :], PS[:, TURN, :]).then_inc(f_ith, 1)
                elif what == "L":
                    t, = args
                    act.wait_ge(f_ld, t + 1)
                    s.copy(LT[:, :], PS[0:E, LOGIT, 0:P]).then_inc(f_lt, 1)
                elif what == "LL":
                    t, = args
                    act.wait_ge(f_dd, t + 1)
                    s.activation(DE[:, :], DD[:, :], ACT.Exp).then_inc(f_de, 1)

        @block.tensor
        def _(pe):
            mm, transpose = nc.tensor.matmul, nc.tensor.transpose

            def job_read(what, t, p=0):
                if what == "K":
                    pe.wait_ge(d_st, 2 * t + 2)
                elif what == "S":
                    pe.wait_ge(d_max, 2 * t + p + 1)
                else:
                    pe.wait_ge(a_exp, 2 * t + p + 1)

            def free_pair(*job):
                before = job_before(*job)
                if before:
                    job_read(*before)
                elif pair_bank(*job) == PAIRS[1]:
                    pe.wait_ge(a_x1, 1)
                return pair_bank(*job)

            def tap(bank, h, k):
                return mm(PS[:, bank, :].rearrange("p (b t) -> p b t", b=HB), DIAG[:, k, :],
                          XT[:, HB * h:HB * h + HB, k:k + P], start=k == 0, stop=k == TAPS - 1)

            def project(bank, w, xt, t, cols, n):
                for g in range(NG):
                    c = slice(g * P, (g + 1) * P)
                    mm(PS[:, bank, c], w[:, g, :], xt[:, t * P:(t + 1) * P], start=True, stop=False)
                    tokens = A_T + t * P
                    last = mm(PS[:, bank, c], AUX[0:n, cols + g * P:cols + (g + 1) * P],
                              AUX[0:n, tokens:tokens + P], start=False, stop=True)
                return last

            for x in plan:
                what, args = x[0], x[1:]
                if what == "GC":
                    pe.wait_ge(ld_x, NLX)
                    pe.wait_ge(c_dg, TAPS)
                    pe.wait_ge(c_id, 1)
                    for k in range(TAPS):
                        last = tap(B_GC[0], 0, k)
                    last.then_inc(pe_gc, 1)
                elif what == "C1":
                    k, = args
                    if k == TAPS:
                        pe.wait_ge(c_dgc, TAPS)
                    last = tap(B_CC, 1, k - TAPS) if k >= TAPS else tap(B_GC[1], 1, k)
                    if k == TAPS - 1:
                        last.then_inc(pe_gc, 1)
                    elif k == 2 * TAPS - 1:
                        last.then_inc(pe_cc, 1)
                elif what == "K":
                    t, = args
                    if t == 0:
                        pe.wait_ge(ld_k, NLK)
                        pe.wait_ge(c_aux, 4)
                    b = free_pair("K", t)
                    project(b, WK, CT, t, A_K, A_ROWS).then_inc(pe_p, 1)
                elif what == "Q":
                    t, = args
                    pe.wait_ge(a_x1, t // HB + 1)
                    if t == 0:
                        pe.wait_ge(c_dve, 2)
                    project(pair_bank("K", t) + 1, WQ, X1T, t, A_Q, A_QROWS).then_inc(pe_p, 1)
                elif what == "V":
                    t, = args
                    if t == 1:
                        pe.wait_ge(d_vb, 1)
                    elif t:
                        pe.wait_ge(d_lg, t - 1)
                    mm(PS[:, ONE, 3 * P:4 * P], CT[:, t * P:(t + 1) * P], WV[:, :], start=True, stop=True)\
                        .then_inc(pe_v, 1)
                elif what == "O":
                    h, = args
                    pe.wait_ge(ld_t, NLT)
                    pe.wait_ge(a_tg, h + 1)
                    pe.wait_ge(a_tc, h + 1)
                    for i in range(HB):
                        pe.wait_ge(d_ht, HB * h + i + 1)
                        last = mm(PS[:, B_O[h], i * P:(i + 1) * P], CAND[:, i * P:(i + 1) * P], OW[:, :],
                                  start=True, stop=True)
                    last.then_inc(pe_o, 1)
                elif what == "X1":
                    h, = args
                    pe.wait_ge(d_y, h + 1)
                    for i in range(HB):
                        pe.wait_ge(d_x1, HB * h + i + 1)
                        last = transpose(PS[:, B_O[h], i * P:(i + 1) * P], Y[:, HB * h + i, :], ID[:, :])
                    last.then_inc(pe_x1, 1)
                elif what == "S":
                    t, p = args
                    pe.wait_ge(d_st, 2 * t + 2)
                    b = free_pair(*x)
                    for s in range(2):
                        mm(PS[:, b + s, :].rearrange("p (g k) -> p g k", g=NG), IDB[:, :],
                           CM[:, None, :].broadcast_to([P, NG, P]), start=True, stop=False, skip_group_check=True)
                    for g in range(NG):
                        for s in range(2):
                            r = 32 * (2 * p + s)
                            last = mm(PS[:, b + s, g * P:(g + 1) * P], QS[r:r + 32, t % 2, g, :],
                                      KS[r:r + 32, t % 2, g, :],
                                      start=False, stop=g == NG - 1, skip_group_check=True)
                    last.then_inc(pe_s, 1)
                elif what == "A":
                    t, = args
                    pe.wait_ge(d_nms, t + 1)
                    pe.wait_ge(d_vb, min(t + 2, B))
                    if t == B - 1:
                        pe.wait_ge(d_lg, t)
                    for g in range(NG):
                        last = transpose(PS[:, ONE, g * P:(g + 1) * P], NMS[:, g, :], ID[:, :])
                    last.then_inc(pe_aug, 1)
                elif what == "ST":
                    t, p = args
                    pe.wait_ge(d_qsa, t + 1)
                    b = free_pair(*x)
                    for g in range(NG):
                        for s in range(2):
                            r = 32 * (2 * p + s)
                            last = mm(PS[:, b + s, g * P:(g + 1) * P], KS[r:r + 32, t % 2, g, :],
                                      QSA[r:r + 32, g, :], start=True, stop=True)
                    last.then_inc(pe_st, 1)
                elif what == "PV":
                    t, p = args
                    pe.wait_ge(p_sel, 2 * t + p + 1)
                    if p == 0:
                        pe.wait_ge(p_vm, t + 1)
                    for s in (2 * p, 2 * p + 1):
                        for g in range(NG):
                            mm(PS[32 * g:32 * g + 32, ONE, 0:P], VM[:, t % 2, s, 32 * g:32 * g + 32], PT[:, s, g, :],
                               start=s == 0, stop=s == NS - 1, skip_group_check=True)
                        for g in range(NG):
                            last = mm(PS[32 * g:32 * g + 32, ONE, P:2 * P],
                                      RO[:, R_HM + s * P + 32 * g:R_HM + s * P + 32 * g + 32], PT[:, s, g, :],
                                      start=False, stop=s == NS - 1, skip_group_check=True)
                    last.then_inc(pe_pv, 1)
                elif what == "WO":
                    t, = args
                    if t == 0:
                        pe.wait_ge(ld_q, 32)
                    pe.wait_ge(d_ot, t + 1)
                    mm(PS[:, ONE, 2 * P:3 * P], OT[:, :], WP[:, :], start=True, stop=True).then_inc(pe_wo, 1)
                elif what == "X2":
                    t, = args
                    pe.wait_ge(d_x2, t + 1)
                    transpose(PS[:, ONE, 0:P], X[:, t, :], ID[:, :]).then_inc(pe_x2, 1)
                elif what == "LG":
                    t, = args
                    pe.wait_ge(a_x2, t + 1)
                    mm(PS[:, ONE, P:P + 2 * E], X2T[:, :], RGU[:, :], start=True, stop=True).then_inc(pe_lg, 1)
                elif what == "T":
                    k, = args
                    pe.wait_ge(f_xe, k + 1)
                    if k:
                        pe.wait_ge(f_l, k)
                    else:
                        job_read(*[j for j in jobs if pair_bank(*j) == PAIRS[1]][-1])
                    if k % 4 == 0 and k >= 8:
                        pe.wait_ge(f_itl, k // 4 - 1)
                    for e in range(4):
                        last = transpose(PS[:, TURN, e * P:(e + 1) * P], XE[:, k % 2, e, :], ID[:, :])
                    last.then_inc(f_t, 1)
                elif what in ("G", "U"):
                    t, e = args
                    r = int(what == "U")
                    if t == 0 and e == 0:
                        for q in w_lo:
                            pe.wait_ge(q, 2 * (r + 1))
                    if r == 1 and e == 0 and t == 0:
                        pe.wait_ge(a_tg, 2)
                    if r == 1 and e == 0 and t == 1:
                        pe.wait_ge(a_x1, 2)
                    if e % 4 == 0:
                        pe.wait_ge(f_l, 4 * t + 2 * r + e // 4 + 1)
                    if e == 0 and t >= 1 + r:
                        if r == 0:
                            pe.wait_ge(f_int, t)
                        else:
                            pe.wait_ge(f_a0, t - 1)
                    cut = slice(e * P, (e + 1) * P)
                    for n, (a, w) in enumerate(((XH, WH), (XH, WL), (XL, WH))):
                        last = mm(PS[:, product_bank(t, r), :], a[:, r, cut], w[:, r, e * I:(e + 1) * I],
                                  start=e == 0 and n == 0, stop=e == E - 1 and n == 2)
                    if e == E - 1:
                        last.then_inc(f_u if r else f_g, 1)
                elif what == "IT":
                    t, = args
                    pe.wait_ge(f_int, t + 1)
                    if t + 1 < B:
                        pe.wait_ge(f_l, 4 * t + 8)
                    for c in range(IC):
                        last = transpose(PS[:, TURN, c * P:(c + 1) * P], INT[:, c * P:(c + 1) * P], ID[:, :])
                    last.then_inc(f_it, 1)
                elif what == "L":
                    t, = args
                    pe.wait_ge(f_itl, t + 1)
                    if t:
                        pe.wait_ge(f_lg, t)
                    for c in range(IC):
                        for n, (w, a) in enumerate(((RDH, ITH), (RDL, ITH), (RDH, ITL))):
                            last = mm(PS[0:E, LOGIT, 0:P], w[:, c * E:(c + 1) * E], a[:, c * P:(c + 1) * P],
                                      start=c == 0 and n == 0, stop=c == IC - 1 and n == 2)
                    last.then_inc(f_ld, 1)
                elif what == "LL":
                    t, = args
                    pe.wait_ge(f_lt, t + 1)
                    transpose(PS[:, LOGIT, P:P + E], LT[:, :], ID[0:E, 0:E]).then_inc(f_ll, 1)
                elif what == "D":
                    t, half, c = args
                    if c == 0:
                        if half == 0:
                            pe.wait_ge(f_itl, t + 1)
                            if t:
                                pe.wait_ge(f_acc, t)
                            for q in w_lo:
                                pe.wait_ge(q, NCH // 2)
                        elif t + 1 < B:
                            pe.wait_ge(f_sg, t + 2)
                    o = c * E * P + half * 512
                    cut = slice(c * P, (c + 1) * P)
                    for n, (a, w) in enumerate(((ITH, WH), (ITH, WL), (ITL, WH))):
                        last = mm(PS[:, product_bank(t + 1, 2 + half), :], a[:, cut], w[:, 2, o:o + 512],
                                  start=c == 0 and n == 0, stop=c == IC - 1 and n == 2)
                    if c == IC - 1:
                        last.then_inc(f_d1 if half else f_d0, 1)

        @block.vector
        def _(dve):
            v = nc.vector
            nd = [0]

            def step(ins):
                nd[0] += 1
                ins.then_inc(dv, 1)
                return nd[0]

            def link(ins):
                dve.wait_ge(dv, step(ins))

            def stack(j, S, bank):
                dve.wait_ge(a_low, j + 1)
                v.tensor_tensor(S.rearrange("p g t -> p (g t)"), PS[:, bank, :], LOW[:, j % 2, :].bitcast(F32),
                                ALU.subtract).then_inc(d_st, 1)

            dve.wait_ge(ld_x, NLX)
            dve.wait_ge(c_id, 2)
            for k in range(TAPS):
                v.tensor_scalar(DIAG[:, k, :], ID[:, :], CO[:, C_GW + k:C_GW + k + 1], None, ALU.mult)\
                    .then_inc(c_dg, 1)
            v.tensor_scalar(HGB[:, :], CO[:, C_GB:C_GB + 1], 0.5, None, ALU.mult).then_inc(c_dve, 1)

            for x in plan:
                what, args = x[0], x[1:]
                if what == "W" and split_by_dve(args[0]):
                    c, = args
                    w, o = chunk(c)
                    dve.wait_ge(w_hi[c % 2], c // 2 + 1)
                    v.tensor_tensor(WL[:, w, o:o + WCH], RAW[:, c % 2, :], WH[:, w, o:o + WCH].bitcast(F32),
                                    ALU.subtract).then_inc(w_lo[c % 2], 1)
                elif what == "GC":
                    acc = CAND[:, :].rearrange("p (b t) -> p b t", b=HB)
                    for k in range(TAPS):
                        xs = XT[:, 0:HB, k:k + P]
                        wk = CO[:, C_CW + k:C_CW + k + 1]
                        if k == 0:
                            link(v.tensor_scalar(acc, xs, wk, None, ALU.mult))
                        elif k < TAPS - 1:
                            link(v.scalar_tensor_tensor(acc, xs, wk, acc, ALU.mult, ALU.add))
                        else:
                            v.scalar_tensor_tensor(acc, xs, wk, acc, ALU.mult, ALU.add).then_inc(d_cand, 1)
                    dve.wait_ge(ld_q, 32)
                    v.tensor_scalar(WQ[:, :, :], WQ[:, :, :], SCALE, None, ALU.mult).then_inc(c_dve, 1)
                elif what == "AX":
                    dve.wait_ge(c_aux, 3)
                    v.tensor_tensor(AUX[:, :], AUX_RAW, AUX_LOW.bitcast(F32), ALU.subtract).then_inc(c_aux, 1)
                elif what == "RD":
                    dve.wait_ge(ld_t, NLT)
                    v.tensor_copy(RDH[:, :], RD[:, :]).then_inc(c_dve, 1)
                    dve.wait_ge(c_dve, 3)
                    v.tensor_tensor(RDL[:, :], RD[:, :], RDH[:, :].bitcast(F32), ALU.subtract).then_inc(c_dve, 1)
                elif what == "KE":
                    t, = args
                    if t >= 2:
                        dve.wait_ge(pe_st, 2 * (t - 1))
                    stack(2 * t, KS[:, t % 2, :, :], pair_bank("K", t))
                elif what == "QE":
                    t, = args
                    stack(2 * t + 1, QS[:, t % 2, :, :], pair_bank("K", t) + 1)
                elif what == "GT":
                    h, = args
                    dve.wait_ge(a_tg, h + 1)
                    dve.wait_ge(a_tc, h + 1)
                    dve.wait_ge(c_act, 1)
                    link(v.scalar_tensor_tensor(GATE[:, :], GATE[:, :], 1.0, CAND[:, :], ALU.add, ALU.mult))
                    for i in range(HB):
                        v.tensor_tensor_scan(CAND[:, i * P:(i + 1) * P], DEC[:, :].broadcast_to([P, P]),
                                             GATE[:, i * P:(i + 1) * P], 0.0, ALU.mult, ALU.add).then_inc(d_ht, 1)
                elif what == "V":
                    t, = args
                    dve.wait_ge(pe_v, t + 1)
                    if t >= 2:
                        dve.wait_ge(p_vm, t - 1)
                    v.tensor_tensor(VB[:, t % 2, :], PS[:, ONE, 3 * P:4 * P], RO[:, R_BV:R_BV + P], ALU.add)\
                        .then_inc(d_vb, 1)
                elif what == "O":
                    h, = args
                    dve.wait_ge(pe_o, h + 1)
                    dve.wait_ge(p_xb, 1)
                    y = flat(Y[:, HB * h:HB * h + HB, :])
                    v.scalar_tensor_tensor(y, PS[:, B_O[h], :], 0.5, y, ALU.mult, ALU.add).then_inc(d_y, 1)
                elif what == "N1":
                    h, = args
                    tiles = range(HB * h, HB * h + HB)
                    half = slice(HB * h, HB * h + HB)
                    dve.wait_ge(d_y, h + 1)
                    dve.wait_ge(p_rs, h + 1)
                    for i in tiles:
                        c = step(v.scalar_tensor_tensor(Y[:, i, :], Y[:, i, :], RS[:, i:i + 1],
                                                        RO[:, R_NW:R_NW + P], ALU.mult, ALU.mult))
                    dve.wait_ge(dv, c)
                    link(v.tensor_tensor(Y[:, half, :], Y[:, half, :], X[:, half, :], ALU.add))
                    for i in tiles:
                        c = step(v.bn_stats(ST6[:, i - HB * h, :], Y[:, i, :]))
                    dve.wait_ge(dv, c)
                    for i in tiles:
                        m = v.bn_aggr(MV[:, i, :], ST6[:, i - HB * h, :])
                        if i < HB * h + HB - 1:
                            step(m)
                    m.then_inc(d_mv, 1)
                    dve.wait_ge(d_mv, h + 1)
                    dve.wait_ge(p_r1, h + 1)
                    for i in tiles:
                        v.tensor_scalar(Y[:, i, :], Y[:, i, :], MV[:, i, 0:1], RSTD[:, i:i + 1],
                                        ALU.subtract, ALU.mult).then_inc(d_x1, 1)
                elif what == "S":
                    t, p = args
                    b = pair_bank(*x)
                    dve.wait_ge(pe_s, 2 * t + p + 1)
                    v.tensor_reduce(NM[:, 2 * p:2 * p + 2, :], PS[:, b:b + 2, :]
                                    .rearrange("q s (g k) -> q s g k", g=NG), AX_X, ALU.max, negate=True)\
                        .then_inc(d_max, 1)
                elif what == "NM":
                    t, = args
                    dve.wait_ge(d_max, 2 * t + 2)
                    nm = NMS[:, :, :].rearrange("q g (s r) -> q s g r", s=NS)
                    dve.wait_ge(c_id, 5)
                    if t:
                        dve.wait_ge(pe_aug, t)
                    link(v.tensor_copy(nm[:, :, :, MAX_HI].bitcast(F32R), NM[:, :, :]))
                    v.tensor_tensor(nm[:, :, :, MAX_LO], NM[:, :, :], nm[:, :, :, MAX_HI], ALU.subtract)\
                        .then_inc(d_nms, 1)
                elif what == "A":
                    t, = args
                    dve.wait_ge(pe_aug, t + 1)
                    if t:
                        dve.wait_ge(pe_st, 2 * t)
                    v.tensor_tensor(QSA[:, :, :], PS[:, ONE, :].rearrange("r (g q) -> r g q", g=NG),
                                    QS[:, t % 2, :, :].bitcast(F32), ALU.add).then_inc(d_qsa, 1)
                elif what == "PV" and args[1] == 1:
                    t, _ = args
                    dve.wait_ge(pe_pv, 2 * t + 2)
                    link(v.reciprocal(RC[:, :], PS[:, ONE, P:2 * P]))
                    if t:
                        dve.wait_ge(pe_wo, t)
                    v.tensor_tensor(OT[:, :], PS[:, ONE, 0:P], RC[:, :], ALU.mult).then_inc(d_ot, 1)
                elif what == "WO":
                    t, = args
                    dve.wait_ge(pe_wo, t + 1)
                    dve.wait_ge(p_x1b, t // HB + 1)
                    v.tensor_tensor(Y[:, t, :], PS[:, ONE, 2 * P:3 * P], Y[:, t, :], ALU.add).then_inc(d_z, 1)
                    dve.wait_ge(d_z, t + 1)
                    link(v.bn_stats(ZST[:, :], Y[:, t, :]))
                    v.bn_aggr(ZMV[:, :], ZST[:, :]).then_inc(d_mv2, 1)
                elif what == "N2":
                    t, = args
                    dve.wait_ge(d_mv2, t + 1)
                    dve.wait_ge(p_r2, t + 1)
                    v.tensor_scalar(X[:, t, :], Y[:, t, :], ZMV[:, 0:1], ZR[:, :], ALU.subtract, ALU.mult)\
                        .then_inc(d_x2, 1)
                elif what == "LG":
                    t, = args
                    dve.wait_ge(pe_lg, t + 1)
                    v.tensor_copy(LG[:, :, :], PS[:, ONE, P:P + 2 * E].rearrange("p (a e) -> p a e", e=E))\
                        .then_inc(d_lg, 1)
                    dve.wait_ge(d_lg, t + 1)
                    for a in range(2):
                        c = step(v.max(V8[:, a, :], LG[:, a, :]))
                    dve.wait_ge(dv, c)
                    if t:
                        dve.wait_ge(a_ex, t)
                    v.tensor_tensor(DV[:, :], V8[:, :, 1], V8[:, :, 0], ALU.subtract).then_inc(d_dv, 1)
                    for a in range(2):
                        c = step(v.max_index(I8[:, a, :], V8[:, a, :], LG[:, a, :]))
                    dve.wait_ge(dv, c)
                    link(v.tensor_copy(IF[:, :, :], I8[:, :, 0:2]))
                    iota = RO[:, None, R_IO:R_IO + E].broadcast_to([P, 2, E])
                    cg = CGU[:, t, :, :]

                    def wide(ap):
                        return ap.broadcast_to([P, 2, E])

                    step(v.tensor_tensor(OH[:, :, :], iota, wide(IF[:, :, 1:2]), ALU.is_equal))
                    step(v.tensor_tensor(cg, iota, wide(IF[:, :, 0:1]), ALU.is_equal))
                    dve.wait_ge(a_ex, t + 1)
                    link(v.tensor_scalar(SM[:, :], EX[:, :], 1.0, None, ALU.add))
                    link(v.reciprocal(P0[:, :], SM[:, :]))
                    step(v.tensor_tensor(cg, cg, wide(P0[:, :, None]), ALU.mult))
                    link(v.tensor_tensor(P1[:, :], EX[:, :], P0[:, :], ALU.mult))
                    link(v.tensor_tensor(OH[:, :, :], OH[:, :, :], wide(P1[:, :, None]), ALU.mult))
                    v.tensor_tensor(cg, cg, OH[:, :, :], ALU.add).then_inc(d_cgu, 1)
                elif what == "T":
                    k, = args
                    r, q = k // 2 % 2, k % 2
                    dve.wait_ge(f_h, k + 1)
                    c = slice(q * 512, q * 512 + 512)
                    v.tensor_tensor(XL[:, r, c], PS[:, TURN, :], XH[:, r, c].bitcast(F32), ALU.subtract)\
                        .then_inc(f_l, 1)
                elif what == "G" and args[1] == E - 1:
                    t = args[0]
                    dve.wait_ge(f_th, t + 1)
                    v.scalar_tensor_tensor(TH[:, :], TH[:, :], 1.0, PS[:, product_bank(t, 0), :], ALU.add, ALU.mult)\
                        .then_inc(f_sg, 1)
                elif what == "U" and args[1] == E - 1:
                    t = args[0]
                    dve.wait_ge(f_sg, t + 1)
                    dve.wait_ge(f_u, t + 1)
                    if t:
                        dve.wait_ge(f_it, t)
                    v.scalar_tensor_tensor(INT[:, :], TH[:, :], 0.5, PS[:, product_bank(t, 1), :], ALU.mult, ALU.mult)\
                        .then_inc(f_int, 1)
                elif what == "IT":
                    t, = args
                    dve.wait_ge(f_ith, t + 1)
                    v.tensor_tensor(ITL[:, :], PS[:, TURN, :], ITH[:, :].bitcast(F32), ALU.subtract).then_inc(f_itl, 1)
                elif what == "LL":
                    t, = args
                    dve.wait_ge(f_ll, t + 1)
                    v.tensor_copy(DLG[:, :], PS[:, LOGIT, P:P + E]).then_inc(f_lg, 1)
                    dve.wait_ge(f_lg, t + 1)
                    link(v.max(DV8[:, :], DLG[:, :]))
                    v.tensor_tensor(DD[:, :], DV8[:, 1:2], DV8[:, 0:1], ALU.subtract).then_inc(f_dd, 1)
                    link(v.max_index(DI8[:, :], DV8[:, :], DLG[:, :]))
                    step(v.tensor_copy(DIF[:, :], DI8[:, 0:2]))
                    dve.wait_ge(f_de, t + 1)
                    link(v.tensor_scalar(DS[:, :], DE[:, :], 1.0, None, ALU.add))
                    link(v.reciprocal(DP[:, 0:1], DS[:, :]))
                    link(v.tensor_tensor(DP[:, 1:2], DE[:, :], DP[:, 0:1], ALU.mult))
                    for j in range(2):
                        c = step(v.tensor_scalar(DC[:, j, :], RO[:, R_IO:R_IO + E], DIF[:, j:j + 1], DP[:, j:j + 1],
                                                 ALU.is_equal, ALU.mult))
                    dve.wait_ge(dv, c)
                    link(v.tensor_tensor(CD[:, :], DC[:, 0, :], DC[:, 1, :], ALU.add))
                elif what == "D" and args[2] == IC - 1:
                    t, half, _ = args
                    dve.wait_ge(f_d1 if half else f_d0, t + 1)
                    if half:
                        dve.wait_ge(f_a0, t + 1)
                    for j in range(4):
                        e = 4 * half + j
                        src = X[:, t, :] if e == 0 else YD[:, (e - 1) % 2, :]
                        ins = v.scalar_tensor_tensor(YD[:, e % 2, :],
                                                     PS[:, product_bank(t + 1, 2 + half), j * P:(j + 1) * P],
                                                     CD[:, e:e + 1], src, ALU.mult, ALU.add)
                        if j < 3:
                            link(ins)
                        else:
                            ins.then_inc(f_acc if half else f_a0, 1)
                elif what == "F":
                    t, = args
                    y = YD[:, (E - 1) % 2, :]
                    dve.wait_ge(f_acc, t + 1)
                    link(v.bn_stats(S6[:, :], y))
                    v.bn_aggr(M2[:, :], S6[:, :]).then_inc(f_mv, 1)
                    dve.wait_ge(f_mv, t + 1)
                    dve.wait_ge(f_r, t + 1)
                    if t >= 2:
                        dve.wait_ge(st[t % 2], 16 * (t // 2))
                    v.tensor_scalar(OUT[:, t % 2, :], y, M2[:, 0:1], R1[:, :], ALU.subtract, ALU.mult)\
                        .then_inc(f_out, 1)


def kernel(**inputs):
    import numpy as np
    import concourse.bacc as bacc
    from concourse.bass_utils import run_bass_kernel_spmd

    a = {k: np.asarray(v) for k, v in inputs.items()}

    def c(v):
        return np.ascontiguousarray(v)

    r = np.arange(P)
    slot, row = r // 32, r % 32
    used = row < 3 * DH

    def stacked(w):
        g = np.arange(NG)[:, None]
        idx = (NS * g + slot[None, :]) * DH + (row % DH)[None, :]
        return np.where(used, w[..., idx], np.float32(0))

    def marks(*which):
        return np.isin(row, which).astype(np.float32)[:, None]

    cols = np.concatenate([
        a["L0_attn_gate_w"][:, 0, :], a["L0_attn_cand_w"][:, 0, :],
        a["L0_attn_gate_b"][:, None], a["L0_attn_cand_b"][:, None], a["L0_attn_log_decay"][:, None],
        marks(*range(LO_HI, LO_HI + DH)), marks(*range(HI_LO, HI_LO + DH), MASK_LO),
        np.where(np.arange(P) < 2, np.float32(SCALE), np.float32(1))[:, None],
        (np.arange(P) == 1).astype(np.float32)[:, None],
        (np.arange(P) == 4).astype(np.float32)[:, None]], axis=1)

    def for_groups(v):
        return np.tile(v[:, 0], NG)

    bq, bk, mask = stacked(a["L0_xattn_bq"]).reshape(-1), stacked(a["L0_xattn_bk"]).reshape(-1), \
        a["mask_BxS2_ff0"].reshape(-1)
    mask_rows, max_rows = for_groups(marks(MASK_HI, MASK_LO)), for_groups(marks(MAX_HI, MAX_LO))
    none, one = np.zeros(NG * P, np.float32), np.ones(B * P, np.float32)
    aux = np.concatenate([
        np.stack([bk, bk, max_rows, mask_rows, mask_rows]),
        np.stack([bq, bq, mask_rows, none, none]),
        np.stack([one, one, one, mask, mask])], axis=1)
    head_mask = (r[None, :] % 32 // DH == np.arange(NS)[:, None]).astype(np.float32)
    rows = np.concatenate([
        a["L0_attn_out_b"], a["L0_attn_norm_w"], a["L0_xattn_bv"], a["L0_xattn_bp"],
        head_mask.reshape(-1), np.arange(E, dtype=np.float32)])
    arrays = {
        "x_tok": c(a["x"].transpose(1, 0, 2)),
        "x_t": c(a["x"].transpose(2, 0, 1)),
        "ctx_t": c(a["ctx_1024"].transpose(2, 0, 1).reshape(P, B * P)),
        "cols": c(cols),
        "rows": c(rows),
        "aux": c(aux),
        "out_w": c(a["L0_attn_out_w"].T),
        "w_q": c(stacked(a["L0_xattn_Wq"])),
        "w_k": c(stacked(a["L0_xattn_Wk"])),
        "w_v": c(a["L0_xattn_Wv"]),
        "w_p": c(a["L0_xattn_Wp"]),
        "r_gu": c(np.concatenate([a["L0_ffn_router_gate"], a["L0_ffn_router_up"]]).T),
        "r_down": c(a["L0_ffn_router_down"].reshape(E, IC, P).transpose(2, 1, 0).reshape(P, IC * E)),
        "w_gate": c(a["L0_ffn_w_gate"].transpose(2, 0, 1).reshape(P, E * I)),
        "w_up": c(a["L0_ffn_w_up"].transpose(2, 0, 1).reshape(P, E * I)),
        "w_down": c(a["L0_ffn_w_down"].reshape(E, P, IC, P).transpose(3, 2, 0, 1).reshape(P, IC * E * P)),
    }
    nc = bacc.Bacc("TRN2", target_bir_lowering=False, num_devices=1)
    args = [nc.dram_tensor(n, v.shape, mybir.dt.from_np(v.dtype), kind="ExternalInput").ap() for n, v in arrays.items()]
    out = nc.dram_tensor("y_out", (B, P, P), F32, kind="ExternalOutput").ap()
    decoder_layer(nc, *args, out)
    result = run_bass_kernel_spmd(nc, [arrays], core_ids=[0])
    return result.results[0]["y_out"]
```

```python
from contextlib import ExitStack

import concourse.bass as bass
from concourse import mybir

F32 = mybir.dt.float32
F32R = mybir.dt.float32r
BF16 = mybir.dt.bfloat16
U32 = mybir.dt.uint32
ALU = mybir.AluOpType
ACT = mybir.ActivationFunctionType
AX_X = mybir.AxisListType.X

P = 128
B = 8
HB = 4
TAPS = 7
PAD = TAPS // 2
ROW = P + 2 * PAD
HEADS, DH = 16, 8
NG = 4
NS = 4
E = 8
I = 512
IC = I // P
SCALE = float(DH) ** -0.5
RMS_EPS = 1.1920929e-07
LN_EPS = 1e-05
WCH = 1024
NCH = 3 * E * I // WCH
WBUF = 3
CPW = E * I // WCH
CAUSAL = -3.3895313892515355e38

C_GW, C_CW, C_GB, C_CB, C_LD = 0, TAPS, 2 * TAPS, 2 * TAPS + 1, 2 * TAPS + 2
C_QLOW = C_LD + 1
C_KLOW = C_QLOW + 1
C_AS = C_KLOW + 1
C_AW = C_AS + 1
C_AM = C_AW + 1
NCOL = C_AM + 1
A_ROWS, A_QROWS = 5, 3
A_K, A_Q, A_T = 0, NG * P, 2 * NG * P
A_COLS = 2 * NG * P + B * P
R_OB, R_NW, R_BV, R_BP, R_HM, R_IO = 0, P, 2 * P, 3 * P, 4 * P, 4 * P + NS * P
NROW = R_IO + E
HI_HI, HI_LO, LO_HI, MASK_HI, MASK_LO, MAX_HI, MAX_LO = 0, DH, 2 * DH, 3 * DH, 3 * DH + 1, 3 * DH + 2, 3 * DH + 3



EARLY = [('WM', 9), ('GC',), ('AX',), ('GT', 0), ('W', 0), ('O', 0), ('RD',), ('N1', 0), ('W', 1), ('C1',), ('C1',), ('C1',), ('C1',), ('C1',), ('C1',), ('C1',), ('K', 0), ('N1A', 0), ('W', 2), ('N1B', 0), ('W', 3), ('DC',), ('KE', 0), ('C1',), ('C1',), ('X1', 0), ('C1',), ('V', 0), ('Q', 0), ('QE', 0), ('VM', 0), ('W', 4), ('W', 5), ('C1',), ('S', 0, 0), ('S', 0, 1), ('W', 6), ('NM', 0), ('C1',), ('V', 1), ('A', 0), ('W', 7), ('W', 8), ('C1',), ('ST', 0, 0), ('ST', 0, 1), ('K', 1), ('KE', 1), ('VM', 1), ('PV', 0, 0), ('W', 9), ('PV', 0, 1), ('WO', 0), ('Q', 1), ('W', 11), ('N2', 0), ('W', 10), ('QE', 1), ('X2', 0), ('LG', 0), ('S', 1, 0), ('XE', 0), ('XE', 1), ('C1',), ('T', 0), ('S', 1, 1), ('T', 1), ('XE', 2), ('XE', 3), ('NM', 1), ('V', 2), ('K', 2), ('A', 1), ('Q', 2), ('KE', 2), ('QE', 2)]

TILE_AT = [2.0, 1.5, 2, 2, 2, 5, 5, 6.5, 10.0, 10, 11, 11.5, 12.5, 14, 15, 16.5, 17.5, 19.5, 20.0, 20.5]
SPAN = {1: (-1.5, 10.0), 2: (7, 24)}
BRANCH_AT = [0, 7.6, 10.5, 12, 18, 19.9]


def before_tiles():
    taps = iter(range(2 * TAPS))
    for step in EARLY:
        yield step if step != ("C1",) else ("C1", next(taps))


def tile_plan(t):
    nxt = t + 1
    steps = [("A", t), ("K", nxt), ("Q", nxt), ("KE", nxt), ("QE", nxt), ("VM", nxt), ("ST", t, 0), ("ST", t, 1),
             ("PV", t, 0), ("PV", t, 1), ("S", nxt, 0), ("WO", t), ("S", nxt, 1), ("N2", t), ("NM", nxt),
             ("X2", t), ("LG", t), ("V", t + 2), ("XE", 4 * t), ("XE", 4 * t + 1)]
    steps = list(zip(TILE_AT, steps))
    return [(at, step) for at, step in steps if step[0] == "XE" or step[1] < B]


def expert_plan(t):
    following = t + 1 < B
    if t < B:
        for e in range(E):
            yield ("G", t, e)
            if t >= 2 and e == 2:
                yield ("F", t - 2)
            if t == 1 and e in (0, 2):
                yield ("T", 6 + e // 2)
            if t and e == 4:
                yield ("L", t - 1)
            if t == 0 and e in (1, 3):
                yield ("T", 2 + e // 3)
        for e in range(E):
            yield ("U", t, e)
            if t and e == 1:
                yield ("LL", t - 1)
            if e in (2, 5) and following:
                yield ("T", 4 * t + 4 + e // 3)
    else:
        yield ("L", t - 1)
    if t:
        for half in range(2):
            for c in range(IC):
                yield ("D", t - 1, half, c)
                if t == B and half == 0 and c == 0:
                    yield ("LL", t - 1)
                    yield ("F", t - 2)
                if half == 0 and c in (0, 3) and following:
                    yield ("T", 4 * t + 6 + c // 3)
            if half == 0 and t == B - 1:
                yield ("IT", t)
    if t < B - 1:
        yield ("IT", t)
    elif t == B:
        yield ("F", t - 1)


def schedule():
    per_tile = 3 * E
    attention = []
    for t in range(1, B):
        start, end = SPAN.get(t, (per_tile * (t - 2), per_tile * (t - 1)))
        attention += [(start + (end - start) * at / per_tile, step) for at, step in tile_plan(t)]
    attention += list(zip(BRANCH_AT, [("GT", 1), ("O", 1), ("N1", 1), ("N1A", 1), ("N1B", 1), ("X1", 1)]))
    attention.sort(key=lambda x: x[0])
    plan = list(before_tiles())
    attention = [x for x in attention if x[1] not in plan]
    now = 0
    for t in range(B + 1):
        for step in expert_plan(t):
            if step[0] in "GUD":
                while attention and attention[0][0] <= now:
                    plan.append(attention.pop(0)[1])
                now += 1
            plan.append(step)
            if step[0] == "T" and step[1] % 4 < 2:
                plan.append(("XE", step[1] + 2))
    return plan


def decoder_layer(nc, x_tok, x_t, ctx_t, cols, rows, aux, out_w, w_q, w_k, w_v, w_p,
                  r_gu, r_down, w_gate, w_up, w_down, out):
    with ExitStack() as ctx:
        def sb(name, shape, dt=F32):
            return ctx.enter_context(nc.sbuf_tensor(name, shape, dt))

        def sem(name):
            return ctx.enter_context(nc.semaphore(name))

        XT = sb("XT", [P, B, ROW])
        X = sb("X", [P, B, P])
        CT = sb("CT", [P, B * P])
        AUX = sb("AUX", [A_ROWS, A_COLS], F32R)
        CO = sb("CO", [P, NCOL])
        RO = sb("RO", [P, NROW])
        OW = sb("OW", [P, P])
        WQ = sb("WQ", [P, NG, P])
        WK = sb("WK", [P, NG, P])
        WV = sb("WV", [P, P])
        WP = sb("WP", [P, P])
        RGU = sb("RGU", [P, 2 * E])
        RD = sb("RD", [P, IC * E])
        RDH = sb("RDH", [P, IC * E], F32R)
        RDL = sb("RDL", [P, IC * E], F32R)
        ID = sb("ID", [P, P])
        IDB = sb("IDB", [P, P], BF16)
        CM = sb("CM", [P, P], BF16)
        DIAG = sb("DIAG", [P, TAPS, P])
        DEC = sb("DEC", [P, 1])
        HGB = sb("HGB", [P, 1])
        MHALF = sb("MHALF", [P, HB])
        WH = sb("WH", [P, 3, E * I], F32R)
        WL = sb("WL", [P, 3, E * I], F32R)
        CAND = sb("CAND", [P, HB * P])
        GATE = sb("GATE", [P, HB * P])
        Y = sb("Y", [P, B, P])
        MS = sb("MS", [P, B])
        RS = sb("RS", [P, B])
        ST6 = sb("ST6", [P, HB, 6])
        MV = sb("MV", [P, B, 2])
        RSTD = sb("RSTD", [P, B])
        X1T = sb("X1T", [P, B * P])
        LOW = sb("LOW", [P, 2, NG * P], F32R)
        QS = sb("QS", [P, 2, NG, P], F32R)
        KS = sb("KS", [P, 2, NG, P], F32R)
        QSA = sb("QSA", [P, NG, P], F32R)
        VB = sb("VB", [P, 2, P])
        VM = sb("VM", [P, 2, NS, P])
        NM = sb("NM", [P, NS, NG])
        NMS = sb("NMS", [P, NG, P])
        PT = sb("PT", [P, NS, NG, P])
        RC = sb("RC", [P, P])
        OT = sb("OT", [P, P])
        ZST = sb("ZST", [P, 6])
        ZMV = sb("ZMV", [P, 2])
        ZR = sb("ZR", [P, 1])
        X2T = sb("X2T", [P, P])
        LG = sb("LG", [P, 2, E])
        V8 = sb("V8", [P, 2, 8])
        I8 = sb("I8", [P, 2, 8], U32)
        IF = sb("IF", [P, 2, 2])
        DV = sb("DV", [P, 2])
        EX = sb("EX", [P, 2])
        SM = sb("SM", [P, 2])
        P0 = sb("P0", [P, 2])
        P1 = sb("P1", [P, 2])
        OH = sb("OH", [P, 2, E])
        CGU = sb("CGU", [P, B, 2, E])
        XH = sb("XH", [P, 2, E * P], F32R)
        XL = sb("XL", [P, 2, E * P], F32R)
        ITH = sb("ITH", [P, I], F32R)
        ITL = sb("ITL", [P, I], F32R)
        LT = sb("LT", [E, P])
        DLG = sb("DLG", [P, E])
        DV8 = sb("DV8", [P, 8])
        DI8 = sb("DI8", [P, 8], U32)
        DIF = sb("DIF", [P, 2])
        DD = sb("DD", [P, 1])
        DE = sb("DE", [P, 1])
        DS = sb("DS", [P, 1])
        DP = sb("DP", [P, 2])
        DC = sb("DC", [P, 2, E])
        CD = sb("CD", [P, E])
        S6 = sb("S6", [P, 6])
        M2 = sb("M2", [P, 2])
        R1 = sb("R1", [P, 1])
        ROOM = sb("ROOM", [P, WBUF * WCH])
        RAW = ROOM[:, :].rearrange("p (s c) -> p s c", s=WBUF)
        XE = ROOM[:, 0:1024].rearrange("p (s e t) -> p s e t", s=2, e=4)
        INT = ROOM[:, 1024:1536]
        YD = ROOM[:, 1536:1792].rearrange("p (s t) -> p s t", s=2)
        OUT = ROOM[:, 1792:2048].rearrange("p (s t) -> p s t", s=2)
        TH = ROOM[:, 2048:2560]

        PS = ctx.enter_context(nc.psum_tensor("PS", [P, 8, 512], F32))
        B_GC, B_CC, B_O = [0, 2], 3, [1, 4]
        PAIRS, LATER = [5, 0], 5
        FIRST_JOBS = 7
        ONE = 7
        TURN, LOGIT = 0, 4

        AUX_RAW = PT[0:A_ROWS, :, :, :].rearrange("p a b c -> p (a b c)")
        AUX_LOW = XH[0:A_ROWS, :, :].rearrange("p a b -> p (a b)")

        ld_c = sem("ld_c")
        ld_x = [sem("ld_x0"), sem("ld_x1")]
        ld_a = sem("ld_a")
        ld_k = sem("ld_k")
        ld_t = sem("ld_t")
        ld_q = sem("ld_q")
        ld_w = [sem("ld_w0"), sem("ld_w1"), sem("ld_w2")]
        c_id = sem("c_id")
        c_dg = sem("c_dg")
        c_dve = sem("c_dve")
        c_act = sem("c_act")
        c_dgc = sem("c_dgc")
        c_aux = sem("c_aux")
        dv = sem("dv")
        pl = sem("pl")
        w_hi = [sem("w_hi0"), sem("w_hi1"), sem("w_hi2")]
        w_lo = [sem("w_lo0"), sem("w_lo1"), sem("w_lo2")]
        pe_gc = sem("pe_gc")
        pe_cc = sem("pe_cc")
        pe_p = sem("pe_p")
        pe_v = sem("pe_v")
        pe_o = sem("pe_o")
        pe_x1 = sem("pe_x1")
        pe_s = sem("pe_s")
        pe_aug = sem("pe_aug")
        pe_st = sem("pe_st")
        pe_pv = sem("pe_pv")
        pe_wo = sem("pe_wo")
        pe_x2 = sem("pe_x2")
        pe_lg = sem("pe_lg")
        f_t = sem("f_t")
        f_g = sem("f_g")
        f_u = sem("f_u")
        f_it = sem("f_it")
        f_ld = sem("f_ld")
        f_ll = sem("f_ll")
        f_d0 = sem("f_d0")
        f_d1 = sem("f_d1")
        a_tc = sem("a_tc")
        a_tg = sem("a_tg")
        a_low = sem("a_low")
        a_ms = sem("a_ms")
        a_x1 = sem("a_x1")
        a_exp = sem("a_exp")
        a_x2 = sem("a_x2")
        a_ex = sem("a_ex")
        f_h = sem("f_h")
        f_th = sem("f_th")
        f_ith = sem("f_ith")
        f_lt = sem("f_lt")
        f_de = sem("f_de")
        d_cand = sem("d_cand")
        d_ht = sem("d_ht")
        d_y = sem("d_y")
        d_mv = sem("d_mv")
        d_x1 = sem("d_x1")
        d_st = sem("d_st")
        d_vb = sem("d_vb")
        d_max = sem("d_max")
        d_nms = sem("d_nms")
        d_qsa = sem("d_qsa")
        d_ot = sem("d_ot")
        d_z = sem("d_z")
        d_mv2 = sem("d_mv2")
        d_x2 = sem("d_x2")
        d_lg = sem("d_lg")
        d_dv = sem("d_dv")
        d_cgu = sem("d_cgu")
        f_l = sem("f_l")
        f_sg = sem("f_sg")
        f_int = sem("f_int")
        f_itl = sem("f_itl")
        f_lg = sem("f_lg")
        f_dd = sem("f_dd")
        f_a0 = sem("f_a0")
        f_acc = sem("f_acc")
        f_mv = sem("f_mv")
        f_out = sem("f_out")
        p_xb = sem("p_xb")
        p_rs = sem("p_rs")
        p_r1 = sem("p_r1")
        p_x1b = sem("p_x1b")
        p_vm = sem("p_vm")
        p_sel = sem("p_sel")
        p_r2 = sem("p_r2")
        f_xe = sem("f_xe")
        f_r = sem("f_r")
        st = [sem("st0"), sem("st1")]

        block = ctx.enter_context(nc.Block())
        NLK, NLT = 4 * 16, 4 * 16

        def flat(ap):
            return ap.rearrange("p a b -> p (a b)")

        def product_bank(t, which):
            return 1 + (4 * t + which) % 3

        def turn_bank(k):
            return LOGIT if k in (1, 3) else TURN

        def down_bank(t, half):
            return product_bank(t + 1, 2 + half if t + 1 < B else half)

        def inner(t):
            return (ITH[:, :], ITL[:, :]) if t + 1 < B else (XH[:, 0, 0:I], XL[:, 0, 0:I])

        plan = schedule()
        jobs = [x for x in plan if x[0] in ("K", "S", "ST")]

        def pair_bank(*job):
            n = jobs.index(job)
            return PAIRS[n % 2] if n < FIRST_JOBS else LATER

        def job_before(*job):
            n = jobs.index(job)
            same = [j for j in jobs[:n] if pair_bank(*j) == pair_bank(*job)]
            return same[-1] if same else None

        w_src = [w_gate, w_up, w_down]

        def chunk(c):
            return c // CPW, (c % CPW) * WCH

        def chunks_in(b, n):
            return len(range(b, n, WBUF))

        def split_by_dve(c):
            return c % WBUF == 2 or c == 7

        @block.sync
        def _(sp):
            sp.dma_start(CO[:, :], cols).then_inc(ld_c, 16)
            sp.dma_start(XT[:, 0:HB, PAD:PAD + P], x_t[:, 0:HB, :]).then_inc(ld_x[0], 16)
            sp.dma_start(AUX_RAW, aux).then_inc(ld_a, 16)
            sp.dma_start(CT[:, :], ctx_t).then_inc(ld_k, 16)
            sp.dma_start(WK[:, :, :], w_k).then_inc(ld_k, 16)
            sp.dma_start(WV[:, :], w_v).then_inc(ld_k, 16)
            sp.dma_start(RO[:, :], rows.partition_broadcast(P)).then_inc(ld_k, 16)
            sp.dma_start(XT[:, HB:B, PAD:PAD + P], x_t[:, HB:B, :]).then_inc(ld_x[1], 16)
            for c in range(NCH):
                if c >= WBUF:
                    sp.wait_ge(w_lo[c % WBUF], c // WBUF)
                w, o = chunk(c)
                sp.dma_start(RAW[:, c % WBUF, :], w_src[w][:, o:o + WCH]).then_inc(ld_w[c % WBUF], 16)
            for t in range(B):
                sp.wait_ge(f_out, t + 1)
                sp.dma_start(out[t], OUT[:, t % 2, :]).then_inc(st[t % 2], 16)
            for q in st:
                sp.wait_ge(q, 16 * B // 2)

        @block.gpsimd
        def _(pool):
            g = nc.gpsimd
            steps = [0]

            def step(ins):
                steps[0] += 1
                ins.then_inc(pl, 1)
                return steps[0]

            g.memset(XT[:, :, 0:PAD], 0.0)
            g.memset(XT[:, :, PAD + P:ROW], 0.0).then_inc(c_id, 1)
            step(g.memset(ID[:, :], 0.0))
            n = step(g.memset(CM[:, :], 0.0))
            pool.wait_ge(pl, n)
            g.affine_select(out=ID[:, :], in_=ID[:, :], compare_op=ALU.not_equal, fill=1.0, base=0,
                            pattern=[[-1, P]], channel_multiplier=1).then_inc(c_id, 1)
            g.affine_select(out=CM[:, :], in_=CM[:, :], compare_op=ALU.is_ge, fill=CAUSAL, base=0,
                            pattern=[[-1, P]], channel_multiplier=1).then_inc(c_id, 1)
            pool.wait_ge(c_id, 2)
            g.tensor_copy(IDB[:, :], ID[:, :]).then_inc(c_id, 1)
            g.memset(NMS[:, :, :], 0.0)
            g.memset(MHALF[:, :], -0.5).then_inc(c_id, 1)
            pool.wait_ge(c_id, 5)

            def inv_sqrt(dst, src, scale, eps, n):
                pool.wait_ge(pl, step(g.tensor_scalar(dst, src, scale, eps, ALU.mult, ALU.add)))
                return g.tensor_tensor(dst, dst, MHALF[:, 0:n], ALU.pow)

            pool.wait_ge(ld_k, NLK)
            pool.wait_ge(ld_t, NLT)
            g.tensor_tensor(Y[:, :, :], X[:, :, :], RO[:, None, R_OB:R_OB + P].broadcast_to([P, B, P]), ALU.add)\
                .then_inc(p_xb, 1)

            for x in plan:
                what, args = x[0], x[1:]
                if what == "W" and not split_by_dve(args[0]):
                    c, = args
                    w, o = chunk(c)
                    pool.wait_ge(w_hi[c % WBUF], c // WBUF + 1)
                    g.tensor_tensor(WL[:, w, o:o + WCH], RAW[:, c % WBUF, :], WH[:, w, o:o + WCH].bitcast(F32),
                                    ALU.subtract).then_inc(w_lo[c % WBUF], 1)
                elif what == "N1":
                    h, = args
                    half = slice(HB * h, HB * h + HB)
                    pool.wait_ge(a_ms, HB * (h + 1))
                    inv_sqrt(RS[:, half], MS[:, half], 1.0 / P, RMS_EPS, HB).then_inc(p_rs, 1)
                elif what == "N1B":
                    h, = args
                    half = slice(HB * h, HB * h + HB)
                    pool.wait_ge(d_mv, h + 1)
                    inv_sqrt(RSTD[:, half], MV[:, half, 1], 1.0, LN_EPS, HB).then_inc(p_r1, 1)
                elif what == "Q" and args[0] % HB == 0:
                    h = args[0] // HB
                    pool.wait_ge(pe_x1, h + 1)
                    half = Y[:, HB * h:HB * h + HB, :]
                    g.tensor_tensor(half, half, RO[:, None, R_BP:R_BP + P].broadcast_to([P, HB, P]), ALU.add)\
                        .then_inc(p_x1b, 1)
                elif what == "VM":
                    t, = args
                    pool.wait_ge(d_vb, t + 1)
                    if t >= 2:
                        pool.wait_ge(pe_pv, 2 * (t - 1))
                    g.tensor_tensor(VM[:, t % 2, :, :], VB[:, t % 2, None, :].broadcast_to([P, NS, P]),
                                    RO[:, R_HM:R_HM + NS * P].rearrange("p (s d) -> p s d", s=NS),
                                    ALU.mult).then_inc(p_vm, 1)
                elif what == "ST":
                    t, p = args
                    pool.wait_ge(a_exp, 2 * t + p + 1)
                    v = PT[:, 2 * p:2 * p + 2, :, :].rearrange("k s g q -> k (s g) q")
                    g.affine_select(out=v, in_=v, compare_op=ALU.is_ge, fill=0.0, base=0,
                                    pattern=[[0, 2 * NG], [1, P]], channel_multiplier=-1).then_inc(p_sel, 1)
                elif what == "N2":
                    t, = args
                    pool.wait_ge(d_mv2, t + 1)
                    inv_sqrt(ZR[:, :], ZMV[:, 1:2], 1.0, LN_EPS, 1).then_inc(p_r2, 1)
                elif what == "XE":
                    k, = args
                    t, r, q = k // 4, k // 2 % 2, k % 2
                    if k == 0:
                        for split in w_lo:
                            pool.wait_ge(split, NCH // WBUF)
                    if k >= 2:
                        pool.wait_ge(f_t, k - 1)
                    if k % 4 == 0:
                        pool.wait_ge(d_cgu, t + 1)
                    g.tensor_tensor(XE[:, k % 2, :, :], X[:, t, None, :].broadcast_to([P, 4, P]),
                                    CGU[:, t, r, 4 * q:4 * q + 4, None].broadcast_to([P, 4, P]), ALU.mult)\
                        .then_inc(f_xe, 1)
                elif what == "F":
                    pool.wait_ge(f_mv, args[0] + 1)
                    inv_sqrt(R1[:, :], M2[:, 1:2], 1.0, LN_EPS, 1).then_inc(f_r, 1)

        @block.scalar
        def _(act):
            s = nc.scalar
            act.dma_start(X[:, :, :], x_tok).then_inc(ld_t, 16)
            act.dma_start(OW[:, :], out_w).then_inc(ld_t, 16)
            act.dma_start(RGU[:, :], r_gu).then_inc(ld_t, 16)
            act.dma_start(RD[:, :], r_down).then_inc(ld_t, 16)
            act.dma_start(WQ[:, :, :], w_q).then_inc(ld_q, 16)
            act.dma_start(WP[:, :], w_p).then_inc(ld_q, 16)
            act.wait_ge(ld_c, 16)
            s.activation(DEC[:, :], CO[:, C_LD:C_LD + 1], ACT.Exp).then_inc(c_act, 1)

            def low_rows(j, bank, low):
                act.wait_ge(pe_p, j + 1)
                if j >= 2:
                    act.wait_ge(d_st, j - 1)
                s.activation(LOW[:, j % 2, :], PS[:, bank, :], ACT.Copy, scale=low).then_inc(a_low, 1)

            for x in plan:
                what, args = x[0], x[1:]
                if what == "W":
                    c, = args
                    w, o = chunk(c)
                    act.wait_ge(ld_w[c % WBUF], 16 * (c // WBUF + 1))
                    s.copy(WH[:, w, o:o + WCH], RAW[:, c % WBUF, :]).then_inc(w_hi[c % WBUF], 1)
                elif what == "AX":
                    act.wait_ge(ld_a, 16)
                    aux_q = AUX_RAW[:, A_Q:A_T]
                    s.activation(aux_q, aux_q, ACT.Copy, scale=CO[0:A_ROWS, C_AS:C_AS + 1]).then_inc(c_aux, 1)
                    s.activation(AUX_LOW[:, A_T:A_COLS], AUX_RAW[:, A_T:A_COLS], ACT.Copy,
                                 scale=CO[0:A_ROWS, C_AM:C_AM + 1]).then_inc(c_aux, 1)
                    act.wait_ge(c_aux, 1)
                    s.activation(AUX_LOW[:, 0:A_T], AUX_RAW[:, 0:A_T], ACT.Copy,
                                 scale=CO[0:A_ROWS, C_AW:C_AW + 1]).then_inc(c_aux, 1)
                elif what == "DC":
                    act.wait_ge(pe_gc, 2)
                    for k in range(TAPS):
                        s.activation(DIAG[:, k, :], ID[:, :], ACT.Copy, scale=CO[:, C_CW + k:C_CW + k + 1])\
                            .then_inc(c_dgc, 1)
                elif what == "GT":
                    h, = args
                    if h == 0:
                        act.wait_ge(d_cand, 1)
                        cand = CAND[:, :]
                    else:
                        act.wait_ge(pe_cc, 1)
                        act.wait_ge(pe_o, 1)
                        act.wait_ge(a_ms, HB)
                        cand = PS[:, B_CC, :]
                    s.activation(CAND[:, :], cand, ACT.Tanh, bias=CO[:, C_CB:C_CB + 1]).then_inc(a_tc, 1)
                    act.wait_ge(pe_gc, h + 1)
                    act.wait_ge(c_dve, 1)
                    s.activation(GATE[:, :], PS[:, B_GC[h], :], ACT.Tanh, bias=HGB[:, :], scale=0.5)\
                        .then_inc(a_tg, 1)
                elif what == "KE":
                    t, = args
                    low_rows(2 * t, pair_bank("K", t), CO[:, C_KLOW:C_KLOW + 1])
                elif what == "QE":
                    t, = args
                    low_rows(2 * t + 1, pair_bank("K", t) + 1, CO[:, C_QLOW:C_QLOW + 1])
                elif what == "O":
                    h, = args
                    act.wait_ge(d_y, h + 1)
                    for i in range(HB * h, HB * h + HB):
                        if i:
                            act.wait_ge(a_ms, i)
                        s.activation(GATE[:, 0:P], Y[:, i, :], ACT.Square, accum_out=MS[:, i:i + 1]).then_inc(a_ms, 1)
                elif what == "X1":
                    h, = args
                    act.wait_ge(pe_x1, h + 1)
                    s.copy(X1T[:, HB * P * h:HB * P * (h + 1)], PS[:, B_O[h], :]).then_inc(a_x1, 1)
                elif what == "ST":
                    t, p = args
                    act.wait_ge(pe_st, 2 * t + p + 1)
                    if t:
                        act.wait_ge(pe_pv, 2 * t + p - 1)
                    b = pair_bank(*x)
                    s.activation(PT[:, 2 * p:2 * p + 2, :, :].rearrange("k s g q -> k (s g q)"),
                                 PS[:, b:b + 2, :].rearrange("k s c -> k (s c)"), ACT.Exp).then_inc(a_exp, 1)
                elif what == "X2":
                    t, = args
                    act.wait_ge(pe_x2, t + 1)
                    if t:
                        act.wait_ge(pe_lg, t)
                    s.copy(X2T[:, :], PS[:, ONE, 0:P]).then_inc(a_x2, 1)
                elif what == "LG":
                    t, = args
                    act.wait_ge(d_dv, t + 1)
                    s.activation(EX[:, :], DV[:, :], ACT.Exp).then_inc(a_ex, 1)
                elif what == "T":
                    k, = args
                    r, q = k // 2 % 2, k % 2
                    act.wait_ge(f_t, k + 1)
                    s.copy(XH[:, r, q * 512:q * 512 + 512], PS[:, turn_bank(k), :]).then_inc(f_h, 1)
                elif what == "G" and args[1] == E - 1:
                    t = args[0]
                    act.wait_ge(f_g, t + 1)
                    if t:
                        act.wait_ge(f_int, t)
                    s.activation(TH[:, :], PS[:, product_bank(t, 0), :], ACT.Tanh, scale=0.5).then_inc(f_th, 1)
                elif what == "IT":
                    t, = args
                    act.wait_ge(f_it, t + 1)
                    s.copy(inner(t)[0], PS[:, TURN, :]).then_inc(f_ith, 1)
                elif what == "L":
                    t, = args
                    act.wait_ge(f_ld, t + 1)
                    s.copy(LT[:, :], PS[0:E, LOGIT, 0:P]).then_inc(f_lt, 1)
                elif what == "LL":
                    t, = args
                    act.wait_ge(f_dd, t + 1)
                    s.activation(DE[:, :], DD[:, :], ACT.Exp).then_inc(f_de, 1)

        @block.tensor
        def _(pe):
            mm, transpose = nc.tensor.matmul, nc.tensor.transpose

            def job_read(what, t, p=0):
                if what == "K":
                    pe.wait_ge(d_st, 2 * t + 2)
                elif what == "S":
                    pe.wait_ge(d_max, 2 * t + p + 1)
                else:
                    pe.wait_ge(a_exp, 2 * t + p + 1)

            def free_pair(*job):
                before = job_before(*job)
                if before:
                    job_read(*before)
                elif pair_bank(*job) == PAIRS[1]:
                    pe.wait_ge(a_x1, 1)
                return pair_bank(*job)

            def tap(bank, h, k):
                return mm(PS[:, bank, :].rearrange("p (b t) -> p b t", b=HB), DIAG[:, k, :],
                          XT[:, HB * h:HB * h + HB, k:k + P], start=k == 0, stop=k == TAPS - 1)

            def project(bank, w, xt, t, cols, n):
                for g in range(NG):
                    c = slice(g * P, (g + 1) * P)
                    mm(PS[:, bank, c], w[:, g, :], xt[:, t * P:(t + 1) * P], start=True, stop=False)
                    tokens = A_T + t * P
                    last = mm(PS[:, bank, c], AUX[0:n, cols + g * P:cols + (g + 1) * P],
                              AUX[0:n, tokens:tokens + P], start=False, stop=True)
                return last

            for x in plan:
                what, args = x[0], x[1:]
                if what == "GC":
                    pe.wait_ge(ld_x[0], 16)
                    pe.wait_ge(c_dg, TAPS)
                    pe.wait_ge(c_id, 1)
                    for k in range(TAPS):
                        last = tap(B_GC[0], 0, k)
                    last.then_inc(pe_gc, 1)
                elif what == "WM":
                    pe.wait_ge(c_id, 5)
                    for _ in range(args[0]):
                        mm(PS[:, LOGIT, :].rearrange("p (g k) -> p g k", g=NG), IDB[:, :],
                           CM[:, None, :].broadcast_to([P, NG, P]), start=True, stop=True)
                elif what == "C1":
                    k, = args
                    if k == 0:
                        pe.wait_ge(ld_x[1], 16)
                    if k >= TAPS:
                        pe.wait_ge(c_dgc, k - TAPS + 1)
                    last = tap(B_CC, 1, k - TAPS) if k >= TAPS else tap(B_GC[1], 1, k)
                    if k == TAPS - 1:
                        last.then_inc(pe_gc, 1)
                    elif k == 2 * TAPS - 1:
                        last.then_inc(pe_cc, 1)
                elif what == "K":
                    t, = args
                    if t == 0:
                        pe.wait_ge(ld_k, NLK)
                        pe.wait_ge(c_aux, 4)
                    b = free_pair("K", t)
                    project(b, WK, CT, t, A_K, A_ROWS).then_inc(pe_p, 1)
                elif what == "Q":
                    t, = args
                    pe.wait_ge(a_x1, t // HB + 1)
                    if t == 0:
                        pe.wait_ge(c_dve, 2)
                    project(pair_bank("K", t) + 1, WQ, X1T, t, A_Q, A_QROWS).then_inc(pe_p, 1)
                elif what == "V":
                    t, = args
                    if t == 1:
                        pe.wait_ge(d_vb, 1)
                    elif t:
                        pe.wait_ge(d_lg, t - 1)
                    mm(PS[:, ONE, 3 * P:4 * P], CT[:, t * P:(t + 1) * P], WV[:, :], start=True, stop=True)\
                        .then_inc(pe_v, 1)
                elif what == "O":
                    h, = args
                    pe.wait_ge(ld_t, NLT)
                    if h:
                        pe.wait_ge(f_l, 4)
                    for i in range(HB):
                        pe.wait_ge(d_ht, HB * h + i + 1)
                        last = mm(PS[:, B_O[h], i * P:(i + 1) * P], CAND[:, i * P:(i + 1) * P], OW[:, :],
                                  start=True, stop=True)
                    last.then_inc(pe_o, 1)
                elif what == "X1":
                    h, = args
                    pe.wait_ge(d_y, h + 1)
                    for i in range(HB):
                        pe.wait_ge(d_x1, HB * h + i + 1)
                        last = transpose(PS[:, B_O[h], i * P:(i + 1) * P], Y[:, HB * h + i, :], ID[:, :])
                    last.then_inc(pe_x1, 1)
                elif what == "S":
                    t, p = args
                    pe.wait_ge(d_st, 2 * t + 2)
                    b = free_pair(*x)
                    for s in range(2):
                        mm(PS[:, b + s, :].rearrange("p (g k) -> p g k", g=NG), IDB[:, :],
                           CM[:, None, :].broadcast_to([P, NG, P]), start=True, stop=False, skip_group_check=True)
                    for g in range(NG):
                        for s in range(2):
                            r = 32 * (2 * p + s)
                            last = mm(PS[:, b + s, g * P:(g + 1) * P], QS[r:r + 32, t % 2, g, :],
                                      KS[r:r + 32, t % 2, g, :],
                                      start=False, stop=g == NG - 1, skip_group_check=True)
                    last.then_inc(pe_s, 1)
                elif what == "A":
                    t, = args
                    pe.wait_ge(d_nms, t + 1)
                    pe.wait_ge(d_vb, min(t + 2, B))
                    if t == B - 1:
                        pe.wait_ge(d_lg, t)
                    for g in range(NG):
                        last = transpose(PS[:, ONE, g * P:(g + 1) * P], NMS[:, g, :], ID[:, :])
                    last.then_inc(pe_aug, 1)
                elif what == "ST":
                    t, p = args
                    pe.wait_ge(d_qsa, t + 1)
                    b = free_pair(*x)
                    for g in range(NG):
                        for s in range(2):
                            r = 32 * (2 * p + s)
                            last = mm(PS[:, b + s, g * P:(g + 1) * P], KS[r:r + 32, t % 2, g, :],
                                      QSA[r:r + 32, g, :], start=True, stop=True)
                    last.then_inc(pe_st, 1)
                elif what == "PV":
                    t, p = args
                    pe.wait_ge(p_sel, 2 * t + p + 1)
                    if p == 0:
                        pe.wait_ge(p_vm, t + 1)
                    for s in (2 * p, 2 * p + 1):
                        for g in range(NG):
                            mm(PS[32 * g:32 * g + 32, ONE, 0:P], VM[:, t % 2, s, 32 * g:32 * g + 32], PT[:, s, g, :],
                               start=s == 0, stop=s == NS - 1, skip_group_check=True)
                        for g in range(NG):
                            last = mm(PS[32 * g:32 * g + 32, ONE, P:2 * P],
                                      RO[:, R_HM + s * P + 32 * g:R_HM + s * P + 32 * g + 32], PT[:, s, g, :],
                                      start=False, stop=s == NS - 1, skip_group_check=True)
                    last.then_inc(pe_pv, 1)
                elif what == "WO":
                    t, = args
                    if t == 0:
                        pe.wait_ge(ld_q, 32)
                    pe.wait_ge(d_ot, t + 1)
                    mm(PS[:, ONE, 2 * P:3 * P], OT[:, :], WP[:, :], start=True, stop=True).then_inc(pe_wo, 1)
                elif what == "X2":
                    t, = args
                    pe.wait_ge(d_x2, t + 1)
                    transpose(PS[:, ONE, 0:P], X[:, t, :], ID[:, :]).then_inc(pe_x2, 1)
                elif what == "LG":
                    t, = args
                    pe.wait_ge(a_x2, t + 1)
                    mm(PS[:, ONE, P:P + 2 * E], X2T[:, :], RGU[:, :], start=True, stop=True).then_inc(pe_lg, 1)
                elif what == "T":
                    k, = args
                    pe.wait_ge(f_xe, k + 1)
                    if k >= 2:
                        pe.wait_ge(f_l, max(k - 1, k if k > 4 else 0))
                    if k == 0:
                        job_read(*[j for j in jobs if pair_bank(*j) == PAIRS[1]][-1])
                    if k == 6 or k % 4 == 0 and k >= 8:
                        pe.wait_ge(f_itl, max(k // 4 - 1, 1))
                    for e in range(4):
                        last = transpose(PS[:, turn_bank(k), e * P:(e + 1) * P], XE[:, k % 2, e, :], ID[:, :])
                    last.then_inc(f_t, 1)
                elif what in ("G", "U"):
                    t, e = args
                    r = int(what == "U")
                    if t == 0 and e == 0:
                        for b, q in enumerate(w_lo):
                            pe.wait_ge(q, chunks_in(b, CPW * (r + 1)))
                    if r == 1 and e == 0 and t == 0:
                        pe.wait_ge(a_tg, 2)
                    if r == 1 and e == 0 and t == 1:
                        pe.wait_ge(a_tc, 2)
                    if e % 4 == 0:
                        pe.wait_ge(f_l, 4 * t + 2 * r + e // 4 + 1)
                    if e == 0 and t >= 1 + r:
                        if r == 0:
                            pe.wait_ge(f_int, t)
                        else:
                            pe.wait_ge(f_a0, t - 1)
                    cut = slice(e * P, (e + 1) * P)
                    for n, (a, w) in enumerate(((XH, WH), (XH, WL), (XL, WH))):
                        last = mm(PS[:, product_bank(t, r), :], a[:, r, cut], w[:, r, e * I:(e + 1) * I],
                                  start=e == 0 and n == 0, stop=e == E - 1 and n == 2)
                    if e == E - 1:
                        last.then_inc(f_u if r else f_g, 1)
                elif what == "IT":
                    t, = args
                    pe.wait_ge(f_int, t + 1)
                    if t + 1 < B:
                        pe.wait_ge(f_l, 4 * t + 8 if t else 6)
                    for c in range(IC):
                        last = transpose(PS[:, TURN, c * P:(c + 1) * P], INT[:, c * P:(c + 1) * P], ID[:, :])
                    last.then_inc(f_it, 1)
                elif what == "L":
                    t, = args
                    pe.wait_ge(f_itl, t + 1)
                    if t:
                        pe.wait_ge(f_lg, t)
                    else:
                        pe.wait_ge(a_x1, 2)
                    high, low = inner(t)
                    for c in range(IC):
                        for n, (w, a) in enumerate(((RDH, high), (RDL, high), (RDH, low))):
                            last = mm(PS[0:E, LOGIT, 0:P], w[:, c * E:(c + 1) * E], a[:, c * P:(c + 1) * P],
                                      start=c == 0 and n == 0, stop=c == IC - 1 and n == 2)
                    last.then_inc(f_ld, 1)
                elif what == "LL":
                    t, = args
                    pe.wait_ge(f_lt, t + 1)
                    transpose(PS[:, LOGIT, P:P + E], LT[:, :], ID[0:E, 0:E]).then_inc(f_ll, 1)
                elif what == "D":
                    t, half, c = args
                    high, low = inner(t)
                    if c == 0 and t == B - 1:
                        pe.wait_ge(f_a0 if half else f_itl, B - 1 + (not half))
                    elif c == 0:
                        if half == 0:
                            pe.wait_ge(f_itl, t + 1)
                            if t:
                                pe.wait_ge(f_acc, t)
                            for q in w_lo:
                                pe.wait_ge(q, NCH // WBUF)
                        elif t + 1 < B:
                            pe.wait_ge(f_sg, t + 2)
                    o = c * E * P + half * 512
                    cut = slice(c * P, (c + 1) * P)
                    for n, (a, w) in enumerate(((high, WH), (high, WL), (low, WH))):
                        last = mm(PS[:, down_bank(t, half), :], a[:, cut], w[:, 2, o:o + 512],
                                  start=c == 0 and n == 0, stop=c == IC - 1 and n == 2)
                    if c == IC - 1:
                        last.then_inc(f_d1 if half else f_d0, 1)

        @block.vector
        def _(dve):
            v = nc.vector
            steps = [0]

            def step(ins):
                steps[0] += 1
                ins.then_inc(dv, 1)
                return steps[0]

            def link(ins):
                dve.wait_ge(dv, step(ins))

            def stack(j, S, bank):
                dve.wait_ge(a_low, j + 1)
                v.tensor_tensor(S.rearrange("p g t -> p (g t)"), PS[:, bank, :], LOW[:, j % 2, :].bitcast(F32),
                                ALU.subtract).then_inc(d_st, 1)

            dve.wait_ge(ld_c, 16)
            dve.wait_ge(c_id, 2)
            for k in range(TAPS):
                v.tensor_scalar(DIAG[:, k, :], ID[:, :], CO[:, C_GW + k:C_GW + k + 1], None, ALU.mult)\
                    .then_inc(c_dg, 1)
            v.tensor_scalar(HGB[:, :], CO[:, C_GB:C_GB + 1], 0.5, None, ALU.mult).then_inc(c_dve, 1)

            for x in plan:
                what, args = x[0], x[1:]
                if what == "W" and split_by_dve(args[0]):
                    c, = args
                    w, o = chunk(c)
                    dve.wait_ge(w_hi[c % WBUF], c // WBUF + 1)
                    v.tensor_tensor(WL[:, w, o:o + WCH], RAW[:, c % WBUF, :], WH[:, w, o:o + WCH].bitcast(F32),
                                    ALU.subtract).then_inc(w_lo[c % WBUF], 1)
                elif what == "GC":
                    dve.wait_ge(ld_x[0], 16)
                    acc = CAND[:, :].rearrange("p (b t) -> p b t", b=HB)
                    for k in range(TAPS):
                        xs = XT[:, 0:HB, k:k + P]
                        wk = CO[:, C_CW + k:C_CW + k + 1]
                        if k == 0:
                            link(v.tensor_scalar(acc, xs, wk, None, ALU.mult))
                        elif k < TAPS - 1:
                            link(v.scalar_tensor_tensor(acc, xs, wk, acc, ALU.mult, ALU.add))
                        else:
                            v.scalar_tensor_tensor(acc, xs, wk, acc, ALU.mult, ALU.add).then_inc(d_cand, 1)
                    dve.wait_ge(ld_q, 32)
                    v.tensor_scalar(WQ[:, :, :], WQ[:, :, :], SCALE, None, ALU.mult).then_inc(c_dve, 1)
                elif what == "AX":
                    dve.wait_ge(c_aux, 3)
                    v.tensor_tensor(AUX[:, :], AUX_RAW, AUX_LOW.bitcast(F32), ALU.subtract).then_inc(c_aux, 1)
                elif what == "RD":
                    dve.wait_ge(ld_t, NLT)
                    v.tensor_copy(RDH[:, :], RD[:, :]).then_inc(c_dve, 1)
                    dve.wait_ge(c_dve, 3)
                    v.tensor_tensor(RDL[:, :], RD[:, :], RDH[:, :].bitcast(F32), ALU.subtract).then_inc(c_dve, 1)
                elif what == "KE":
                    t, = args
                    if t >= 2:
                        dve.wait_ge(pe_st, 2 * (t - 1))
                    stack(2 * t, KS[:, t % 2, :, :], pair_bank("K", t))
                elif what == "QE":
                    t, = args
                    stack(2 * t + 1, QS[:, t % 2, :, :], pair_bank("K", t) + 1)
                elif what == "GT":
                    h, = args
                    dve.wait_ge(a_tg, h + 1)
                    dve.wait_ge(a_tc, h + 1)
                    dve.wait_ge(c_act, 1)
                    link(v.scalar_tensor_tensor(GATE[:, :], GATE[:, :], 1.0, CAND[:, :], ALU.add, ALU.mult))
                    for i in range(HB):
                        v.tensor_tensor_scan(CAND[:, i * P:(i + 1) * P], DEC[:, :].broadcast_to([P, P]),
                                             GATE[:, i * P:(i + 1) * P], 0.0, ALU.mult, ALU.add).then_inc(d_ht, 1)
                elif what == "V":
                    t, = args
                    dve.wait_ge(pe_v, t + 1)
                    if t >= 2:
                        dve.wait_ge(p_vm, t - 1)
                    v.tensor_tensor(VB[:, t % 2, :], PS[:, ONE, 3 * P:4 * P], RO[:, R_BV:R_BV + P], ALU.add)\
                        .then_inc(d_vb, 1)
                elif what == "O":
                    h, = args
                    dve.wait_ge(pe_o, h + 1)
                    dve.wait_ge(p_xb, 1)
                    y = flat(Y[:, HB * h:HB * h + HB, :])
                    v.scalar_tensor_tensor(y, PS[:, B_O[h], :], 0.5, y, ALU.mult, ALU.add).then_inc(d_y, 1)
                elif what == "N1":
                    h, = args
                    tiles = range(HB * h, HB * h + HB)
                    half = slice(HB * h, HB * h + HB)
                    dve.wait_ge(d_y, h + 1)
                    dve.wait_ge(p_rs, h + 1)
                    for i in tiles:
                        step(v.scalar_tensor_tensor(Y[:, i, :], Y[:, i, :], RS[:, i:i + 1],
                                                        RO[:, R_NW:R_NW + P], ALU.mult, ALU.mult))
                elif what == "N1A":
                    h, = args
                    tiles = range(HB * h, HB * h + HB)
                    half = slice(HB * h, HB * h + HB)
                    dve.wait_ge(dv, steps[0])
                    link(v.tensor_tensor(Y[:, half, :], Y[:, half, :], X[:, half, :], ALU.add))
                    for i in tiles:
                        c = step(v.bn_stats(ST6[:, i - HB * h, :], Y[:, i, :]))
                    dve.wait_ge(dv, c)
                    for i in tiles:
                        m = v.bn_aggr(MV[:, i, :], ST6[:, i - HB * h, :])
                        if i < HB * h + HB - 1:
                            step(m)
                    m.then_inc(d_mv, 1)
                elif what == "N1B":
                    h, = args
                    tiles = range(HB * h, HB * h + HB)
                    dve.wait_ge(d_mv, h + 1)
                    dve.wait_ge(p_r1, h + 1)
                    for i in tiles:
                        v.tensor_scalar(Y[:, i, :], Y[:, i, :], MV[:, i, 0:1], RSTD[:, i:i + 1],
                                        ALU.subtract, ALU.mult).then_inc(d_x1, 1)
                elif what == "S":
                    t, p = args
                    b = pair_bank(*x)
                    dve.wait_ge(pe_s, 2 * t + p + 1)
                    v.tensor_reduce(NM[:, 2 * p:2 * p + 2, :], PS[:, b:b + 2, :]
                                    .rearrange("q s (g k) -> q s g k", g=NG), AX_X, ALU.max, negate=True)\
                        .then_inc(d_max, 1)
                elif what == "NM":
                    t, = args
                    dve.wait_ge(d_max, 2 * t + 2)
                    nm = NMS[:, :, :].rearrange("q g (s r) -> q s g r", s=NS)
                    dve.wait_ge(c_id, 5)
                    if t:
                        dve.wait_ge(pe_aug, t)
                    link(v.tensor_copy(nm[:, :, :, MAX_HI].bitcast(F32R), NM[:, :, :]))
                    v.tensor_tensor(nm[:, :, :, MAX_LO], NM[:, :, :], nm[:, :, :, MAX_HI], ALU.subtract)\
                        .then_inc(d_nms, 1)
                elif what == "A":
                    t, = args
                    dve.wait_ge(pe_aug, t + 1)
                    if t:
                        dve.wait_ge(pe_st, 2 * t)
                    v.tensor_tensor(QSA[:, :, :], PS[:, ONE, :].rearrange("r (g q) -> r g q", g=NG),
                                    QS[:, t % 2, :, :].bitcast(F32), ALU.add).then_inc(d_qsa, 1)
                elif what == "PV" and args[1] == 1:
                    t, _ = args
                    dve.wait_ge(pe_pv, 2 * t + 2)
                    link(v.reciprocal(RC[:, :], PS[:, ONE, P:2 * P]))
                    if t:
                        dve.wait_ge(pe_wo, t)
                    v.tensor_tensor(OT[:, :], PS[:, ONE, 0:P], RC[:, :], ALU.mult).then_inc(d_ot, 1)
                elif what == "WO":
                    t, = args
                    dve.wait_ge(pe_wo, t + 1)
                    dve.wait_ge(p_x1b, t // HB + 1)
                    v.tensor_tensor(Y[:, t, :], PS[:, ONE, 2 * P:3 * P], Y[:, t, :], ALU.add).then_inc(d_z, 1)
                    dve.wait_ge(d_z, t + 1)
                    link(v.bn_stats(ZST[:, :], Y[:, t, :]))
                    v.bn_aggr(ZMV[:, :], ZST[:, :]).then_inc(d_mv2, 1)
                elif what == "N2":
                    t, = args
                    dve.wait_ge(d_mv2, t + 1)
                    dve.wait_ge(p_r2, t + 1)
                    v.tensor_scalar(X[:, t, :], Y[:, t, :], ZMV[:, 0:1], ZR[:, :], ALU.subtract, ALU.mult)\
                        .then_inc(d_x2, 1)
                elif what == "LG":
                    t, = args
                    dve.wait_ge(pe_lg, t + 1)
                    v.tensor_copy(LG[:, :, :], PS[:, ONE, P:P + 2 * E].rearrange("p (a e) -> p a e", e=E))\
                        .then_inc(d_lg, 1)
                    dve.wait_ge(d_lg, t + 1)
                    for a in range(2):
                        c = step(v.max(V8[:, a, :], LG[:, a, :]))
                    dve.wait_ge(dv, c)
                    if t:
                        dve.wait_ge(a_ex, t)
                    v.tensor_tensor(DV[:, :], V8[:, :, 1], V8[:, :, 0], ALU.subtract).then_inc(d_dv, 1)
                    for a in range(2):
                        c = step(v.max_index(I8[:, a, :], V8[:, a, :], LG[:, a, :]))
                    dve.wait_ge(dv, c)
                    link(v.tensor_copy(IF[:, :, :], I8[:, :, 0:2]))
                    iota = RO[:, None, R_IO:R_IO + E].broadcast_to([P, 2, E])
                    cg = CGU[:, t, :, :]

                    def wide(ap):
                        return ap.broadcast_to([P, 2, E])

                    step(v.tensor_tensor(OH[:, :, :], iota, wide(IF[:, :, 1:2]), ALU.is_equal))
                    step(v.tensor_tensor(cg, iota, wide(IF[:, :, 0:1]), ALU.is_equal))
                    dve.wait_ge(a_ex, t + 1)
                    link(v.tensor_scalar(SM[:, :], EX[:, :], 1.0, None, ALU.add))
                    link(v.reciprocal(P0[:, :], SM[:, :]))
                    step(v.tensor_tensor(cg, cg, wide(P0[:, :, None]), ALU.mult))
                    link(v.tensor_tensor(P1[:, :], EX[:, :], P0[:, :], ALU.mult))
                    link(v.tensor_tensor(OH[:, :, :], OH[:, :, :], wide(P1[:, :, None]), ALU.mult))
                    v.tensor_tensor(cg, cg, OH[:, :, :], ALU.add).then_inc(d_cgu, 1)
                elif what == "T":
                    k, = args
                    r, q = k // 2 % 2, k % 2
                    dve.wait_ge(f_h, k + 1)
                    c = slice(q * 512, q * 512 + 512)
                    v.tensor_tensor(XL[:, r, c], PS[:, turn_bank(k), :], XH[:, r, c].bitcast(F32), ALU.subtract)\
                        .then_inc(f_l, 1)
                elif what == "G" and args[1] == E - 1:
                    t = args[0]
                    dve.wait_ge(f_th, t + 1)
                    v.scalar_tensor_tensor(TH[:, :], TH[:, :], 1.0, PS[:, product_bank(t, 0), :], ALU.add, ALU.mult)\
                        .then_inc(f_sg, 1)
                elif what == "U" and args[1] == E - 1:
                    t = args[0]
                    dve.wait_ge(f_sg, t + 1)
                    dve.wait_ge(f_u, t + 1)
                    if t:
                        dve.wait_ge(f_it, t)
                    v.scalar_tensor_tensor(INT[:, :], TH[:, :], 0.5, PS[:, product_bank(t, 1), :], ALU.mult, ALU.mult)\
                        .then_inc(f_int, 1)
                elif what == "IT":
                    t, = args
                    dve.wait_ge(f_ith, t + 1)
                    high, low = inner(t)
                    v.tensor_tensor(low, PS[:, TURN, :], high.bitcast(F32), ALU.subtract).then_inc(f_itl, 1)
                elif what == "LL":
                    t, = args
                    dve.wait_ge(f_ll, t + 1)
                    v.tensor_copy(DLG[:, :], PS[:, LOGIT, P:P + E]).then_inc(f_lg, 1)
                    dve.wait_ge(f_lg, t + 1)
                    link(v.max(DV8[:, :], DLG[:, :]))
                    v.tensor_tensor(DD[:, :], DV8[:, 1:2], DV8[:, 0:1], ALU.subtract).then_inc(f_dd, 1)
                    link(v.max_index(DI8[:, :], DV8[:, :], DLG[:, :]))
                    step(v.tensor_copy(DIF[:, :], DI8[:, 0:2]))
                    dve.wait_ge(f_de, t + 1)
                    link(v.tensor_scalar(DS[:, :], DE[:, :], 1.0, None, ALU.add))
                    link(v.reciprocal(DP[:, 0:1], DS[:, :]))
                    link(v.tensor_tensor(DP[:, 1:2], DE[:, :], DP[:, 0:1], ALU.mult))
                    for j in range(2):
                        c = step(v.tensor_scalar(DC[:, j, :], RO[:, R_IO:R_IO + E], DIF[:, j:j + 1], DP[:, j:j + 1],
                                                 ALU.is_equal, ALU.mult))
                    dve.wait_ge(dv, c)
                    link(v.tensor_tensor(CD[:, :], DC[:, 0, :], DC[:, 1, :], ALU.add))
                elif what == "D" and args[2] == IC - 1:
                    t, half, _ = args
                    dve.wait_ge(f_d1 if half else f_d0, t + 1)
                    if half:
                        dve.wait_ge(f_a0, t + 1)
                    for j in range(4):
                        e = 4 * half + j
                        src = X[:, t, :] if e == 0 else YD[:, (e - 1) % 2, :]
                        ins = v.scalar_tensor_tensor(YD[:, e % 2, :],
                                                     PS[:, down_bank(t, half), j * P:(j + 1) * P],
                                                     CD[:, e:e + 1], src, ALU.mult, ALU.add)
                        if j < 3:
                            link(ins)
                        else:
                            ins.then_inc(f_acc if half else f_a0, 1)
                elif what == "F":
                    t, = args
                    y = YD[:, (E - 1) % 2, :]
                    dve.wait_ge(f_acc, t + 1)
                    link(v.bn_stats(S6[:, :], y))
                    v.bn_aggr(M2[:, :], S6[:, :]).then_inc(f_mv, 1)
                    dve.wait_ge(f_mv, t + 1)
                    dve.wait_ge(f_r, t + 1)
                    if t >= 2:
                        dve.wait_ge(st[t % 2], 16 * (t // 2))
                    v.tensor_scalar(OUT[:, t % 2, :], y, M2[:, 0:1], R1[:, :], ALU.subtract, ALU.mult)\
                        .then_inc(f_out, 1)


def kernel(**inputs):
    import numpy as np
    import concourse.bacc as bacc
    from concourse.bass_utils import run_bass_kernel_spmd

    a = {k: np.asarray(v) for k, v in inputs.items()}

    def c(v):
        return np.ascontiguousarray(v)

    r = np.arange(P)
    slot, row = r // 32, r % 32
    used = row < 3 * DH

    def stacked(w):
        g = np.arange(NG)[:, None]
        idx = (NS * g + slot[None, :]) * DH + (row % DH)[None, :]
        return np.where(used, w[..., idx], np.float32(0))

    def marks(*which):
        return np.isin(row, which).astype(np.float32)[:, None]

    cols = np.concatenate([
        a["L0_attn_gate_w"][:, 0, :], a["L0_attn_cand_w"][:, 0, :],
        a["L0_attn_gate_b"][:, None], a["L0_attn_cand_b"][:, None], a["L0_attn_log_decay"][:, None],
        marks(*range(LO_HI, LO_HI + DH)), marks(*range(HI_LO, HI_LO + DH), MASK_LO),
        np.where(np.arange(P) < 2, np.float32(SCALE), np.float32(1))[:, None],
        (np.arange(P) == 1).astype(np.float32)[:, None],
        (np.arange(P) == 4).astype(np.float32)[:, None]], axis=1)

    def for_groups(v):
        return np.tile(v[:, 0], NG)

    bq, bk, mask = stacked(a["L0_xattn_bq"]).reshape(-1), stacked(a["L0_xattn_bk"]).reshape(-1), \
        a["mask_BxS2_ff0"].reshape(-1)
    mask_rows, max_rows = for_groups(marks(MASK_HI, MASK_LO)), for_groups(marks(MAX_HI, MAX_LO))
    none, one = np.zeros(NG * P, np.float32), np.ones(B * P, np.float32)
    aux = np.concatenate([
        np.stack([bk, bk, max_rows, mask_rows, mask_rows]),
        np.stack([bq, bq, mask_rows, none, none]),
        np.stack([one, one, one, mask, mask])], axis=1)
    head_mask = (r[None, :] % 32 // DH == np.arange(NS)[:, None]).astype(np.float32)
    rows = np.concatenate([
        a["L0_attn_out_b"], a["L0_attn_norm_w"], a["L0_xattn_bv"], a["L0_xattn_bp"],
        head_mask.reshape(-1), np.arange(E, dtype=np.float32)])
    arrays = {
        "x_tok": c(a["x"].transpose(1, 0, 2)),
        "x_t": c(a["x"].transpose(2, 0, 1)),
        "ctx_t": c(a["ctx_1024"].transpose(2, 0, 1).reshape(P, B * P)),
        "cols": c(cols),
        "rows": c(rows),
        "aux": c(aux),
        "out_w": c(a["L0_attn_out_w"].T),
        "w_q": c(stacked(a["L0_xattn_Wq"])),
        "w_k": c(stacked(a["L0_xattn_Wk"])),
        "w_v": c(a["L0_xattn_Wv"]),
        "w_p": c(a["L0_xattn_Wp"]),
        "r_gu": c(np.concatenate([a["L0_ffn_router_gate"], a["L0_ffn_router_up"]]).T),
        "r_down": c(a["L0_ffn_router_down"].reshape(E, IC, P).transpose(2, 1, 0).reshape(P, IC * E)),
        "w_gate": c(a["L0_ffn_w_gate"].transpose(2, 0, 1).reshape(P, E * I)),
        "w_up": c(a["L0_ffn_w_up"].transpose(2, 0, 1).reshape(P, E * I)),
        "w_down": c(a["L0_ffn_w_down"].reshape(E, P, IC, P).transpose(3, 2, 0, 1).reshape(P, IC * E * P)),
    }
    nc = bacc.Bacc("TRN2", target_bir_lowering=False, num_devices=1)
    args = [nc.dram_tensor(n, v.shape, mybir.dt.from_np(v.dtype), kind="ExternalInput").ap() for n, v in arrays.items()]
    out = nc.dram_tensor("y_out", (B, P, P), F32, kind="ExternalOutput").ap()
    decoder_layer(nc, *args, out)
    result = run_bass_kernel_spmd(nc, [arrays], core_ids=[0])
    return result.results[0]["y_out"]
```
